# Optimizing a Trainium2 kernel written in Bass

```python
import numpy as np
import jax
import jax.numpy as jnp

def _softmax(x, axis=-1):
    return jax.nn.softmax(x, axis=axis)

def _gelu(x):
    return jax.nn.gelu(x, approximate=True)

def _silu(x):
    return jax.nn.silu(x)

def _sigmoid(x):
    return jax.nn.sigmoid(x)

def _layernorm(x, axis=-1, eps=1e-05):
    m = jnp.mean(x, axis=axis, keepdims=True)
    v = jnp.var(x, axis=axis, keepdims=True)
    return (x - m) / jnp.sqrt(v + eps)

def _scatter_add(tgt, idx, src, axis=0):
    return tgt.at[idx].add(src)

def _segment_sum(src, seg, n):
    return jax.ops.segment_sum(src, seg, n)
kernel_name = 'mk_gnn_resnorm_d2_gnn_r64_12c019'

def setup_inputs(seed: int=0):
    np.random.seed(seed)
    _w = jnp.asarray

    def _rec_inputs():
        import jax
        import jax.numpy as jnp
        _gk = jax.random.key(seed)
        x = 7.22e-05 + 1 * jax.random.normal(jax.random.fold_in(_gk, 1), (100000, 64), jnp.float32)
        src = jax.random.randint(jax.random.fold_in(_gk, 2), (50000,), 0, 100000, jnp.int32)
        dst = jnp.minimum((100000 * jax.random.uniform(jax.random.fold_in(_gk, 3), (50000,)) ** 2.0).astype(jnp.int32), 99999)
        _o = jnp.argsort(dst, stable=True)
        src = src[_o]
        dst = dst[_o]
        return (x, src, dst)
    x, src, dst = _rec_inputs()

    def _L0_gnn_setup():
        import jax, jax.numpy as jnp
        import numpy as np
        N = 2048
        IN_DIM = 64
        OUT_DIM = 64
        K = 6
        E = N * K
        key = jax.random.key(seed)
        k1, k2, k3, k4 = jax.random.split(key, 4)
        x = jax.random.normal(k1, (N, IN_DIM), dtype=jnp.float32)
        W = jax.random.normal(k2, (2 * IN_DIM, OUT_DIM), dtype=jnp.float32) / np.sqrt(2 * IN_DIM)
        b = jax.random.normal(k3, (OUT_DIM,), dtype=jnp.float32) * 0.01
        tgt = jnp.repeat(jnp.arange(N, dtype=jnp.int32), K)
        src = jax.random.randint(k4, (E,), 0, N, dtype=jnp.int32)
        edge_index = jnp.stack([tgt, src], axis=0)
        return {'x': x, 'W': W, 'b': b, 'edge_index': edge_index}
    _L0_gnn_all = _L0_gnn_setup()
    _L0_gnn_in = {k: v for k, v in _L0_gnn_all.items() if k in ('W', 'b')}
    del _L0_gnn_all

    def _L1_gnn_setup():
        import jax, jax.numpy as jnp
        import numpy as np
        N_NODES = 100000
        N_EDGES = 25000
        N_CHANNELS = 64
        HIDDEN_DIM = 32
        POLY_DEGREE = 5
        DEG_CLAMP = 1000000.0
        key = jax.random.key(seed)
        k1, k2, k3, k4, k5, k6 = jax.random.split(key, 6)
        x = jax.random.normal(k1, (N_NODES, N_CHANNELS), dtype=jnp.float32)
        edge_index = jax.random.randint(k2, (2, N_EDGES), 0, N_NODES, dtype=jnp.int32)
        fan1 = N_CHANNELS + 4
        W1 = jax.random.uniform(k3, (HIDDEN_DIM, fan1), jnp.float32, -1.0, 1.0) / np.sqrt(fan1)
        b1 = jax.random.uniform(k4, (HIDDEN_DIM,), jnp.float32, -1.0, 1.0) / np.sqrt(fan1)
        W2 = jax.random.uniform(k5, (POLY_DEGREE + 1, HIDDEN_DIM), jnp.float32, -1.0, 1.0) / np.sqrt(HIDDEN_DIM)
        b2 = jax.random.uniform(k6, (POLY_DEGREE + 1,), jnp.float32, -1.0, 1.0) / np.sqrt(HIDDEN_DIM)
        return {'x': x, 'edge_index': edge_index, 'W1': W1, 'b1': b1, 'W2': W2, 'b2': b2}
    _L1_gnn_all = _L1_gnn_setup()
    _L1_gnn_in = {k: v for k, v in _L1_gnn_all.items() if k in ('W1', 'b1', 'W2', 'b2')}
    del _L1_gnn_all
    return {'x': x, 'src': src, 'dst': dst, 'L0_gnn_W': _L0_gnn_in['W'], 'L0_gnn_b': _L0_gnn_in['b'], 'L1_gnn_W1': _L1_gnn_in['W1'], 'L1_gnn_b1': _L1_gnn_in['b1'], 'L1_gnn_W2': _L1_gnn_in['W2'], 'L1_gnn_b2': _L1_gnn_in['b2']}

def reference(x, src, dst, L0_gnn_W, L0_gnn_b, L1_gnn_W1, L1_gnn_b1, L1_gnn_W2, L1_gnn_b2):
    import jax
    import jax.numpy as jnp

    def _L0_gnn_ref(x, W, b, edge_index):
        import jax, jax.numpy as jnp
        import numpy as np
        N = 2048
        IN_DIM = 64
        OUT_DIM = 64
        K = 6
        E = N * K
        tgt = edge_index[0]
        src = edge_index[1]
        x_i = x[tgt]
        x_j = x[src]
        edge_feat = jnp.concatenate([x_i, x_j - x_i], axis=1)
        h = jax.nn.relu(edge_feat @ W + b)
        out = jax.ops.segment_max(h, tgt, num_segments=x.shape[0], indices_are_sorted=True)
        return jnp.maximum(out, 0.0)

    def _L1_gnn_ref(x, edge_index, W1, b1, W2, b2):
        import jax, jax.numpy as jnp
        import numpy as np
        N_NODES = 100000
        N_EDGES = 25000
        N_CHANNELS = 64
        HIDDEN_DIM = 32
        POLY_DEGREE = 5
        DEG_CLAMP = 1000000.0
        N, C = x.shape
        E = edge_index.shape[1]
        row, col = (edge_index[0], edge_index[1])
        deg = jax.ops.segment_sum(jnp.ones((E,), x.dtype), col, num_segments=N)
        deg_inv_sqrt = jnp.minimum(deg ** (-0.5), DEG_CLAMP)
        deg_inv_sqrt = jnp.where(jnp.isinf(deg_inv_sqrt), 0.0, deg_inv_sqrt)
        norm = deg_inv_sqrt[row] * deg_inv_sqrt[col]
        x_mean = x.mean(axis=0)
        stats = jnp.stack([x.mean(), x.std(ddof=1), jnp.asarray(N, x.dtype), jnp.asarray(E, x.dtype)])
        coeff_in = jnp.concatenate([x_mean, stats])
        h = jax.nn.relu(W1 @ coeff_in + b1)
        coeffs = jax.nn.softmax(W2 @ h + b2)
        result = coeffs[0] * x
        tx = x
        for k in range(1, POLY_DEGREE + 1):
            tx = jax.ops.segment_sum(norm[:, None] * tx[col], row, num_segments=N)
            result = result + coeffs[k] * tx
        return result
    edge_index = jnp.stack([src, dst])
    x = _layernorm(x + _L0_gnn_ref(x, L0_gnn_W, L0_gnn_b, edge_index), axis=-1)
    x = _layernorm(x + _L1_gnn_ref(x, edge_index, L1_gnn_W1, L1_gnn_b1, L1_gnn_W2, L1_gnn_b2), axis=-1)
    return x

_drawn_inputs = setup_inputs


def setup_inputs(seed=0):
    import zlib

    import numpy as np

    out = dict(_drawn_inputs(seed))
    spreads = {}
    factors = {'L0_gnn_b': 8.0}
    for name, (base, spread) in spreads.items():
        noise = np.random.default_rng([zlib.crc32(name.encode()), seed]).standard_normal(out[name].shape)
        drawn = base * np.exp(spread * noise) if base else spread * noise
        out[name] = jnp.asarray(drawn.astype(out[name].dtype))
    for name, factor in factors.items():
        out[name] = (out[name] * factor).astype(out[name].dtype)
    return out
```

```python
from contextlib import ExitStack, contextmanager

import concourse.bass as bass
from concourse import mybir

FP32, FP16, BF16 = mybir.dt.float32, mybir.dt.float16, mybir.dt.bfloat16
I32, U32, U8 = mybir.dt.int32, mybir.dt.uint32, mybir.dt.uint8
ALU = mybir.AluOpType
ACT = mybir.ActivationFunctionType
AX = mybir.AxisListType
ds = bass.ds

P = 128
N = 100000
C = 64
E = 50000
HID = 32
NCOEF = 6
EPS = 1e-5
NEG = -1e30
ROUND = 12582912.0
FAR = float(1 << 20)

NP = 125
NC = N // NP
NR = NC // 2
NROW = 2 * NP
BANK = 512

ET = 392
EB = ET // 4
GT = 4
GPOS = GT * P
NG = 100
NT = NG * GT
NPOS = NG * GPOS
assert E + 2 * GPOS <= NPOS
BLK = 4
ZERO_ROW = NPOS
REC = 401 * P
NODE_W = NC * C // 16
TAB_W = (NPOS + P) * C // P // 8
EXT = C + 2
KN = 16
NCH = NC // KN
SPLIT = (0, 112, NP)


def bc(ap, n):
    return ap.unsqueeze(2).to_broadcast([ap.shape[0], ap.shape[1], n])


@contextmanager
def semaphores(nc):
    held = []

    def sem(name):
        held.append(nc.alloc_semaphore(name))
        return held[-1]

    yield sem
    nc.clear_and_free_semaphores(held)
    nc.all_engine_barrier()


class Names:
    pass


class Chain:

    def __init__(self, eng, sem):
        self.eng, self.sem, self.n = eng, sem, 0

    def __call__(self, instruction):
        instruction.then_inc(self.sem, 1)
        self.n += 1
        self.eng.wait_ge(self.sem, self.n)


def settle(eng, k, *values):
    for v in values:
        eng.lower_val(v)
    eng.wait_ge(k.begun, 1)
    return values


def node_dma(eng, sem, dst, src):
    for a, b in zip(SPLIT, SPLIT[1:]):
        eng.dma_start(dst(a, b), src(a, b)).then_inc(sem, 16)


def build(nc, x, src, dst, W0, b0, W1, b1, W2, b2, out):
    def dram(name, shape, dt):
        return nc.dram_tensor(name, shape, dt).ap()

    d = Names()
    d.x, d.src, d.dst, d.out = x, src, dst, out
    d.W0, d.b0, d.W1, d.b1, d.W2, d.b2 = W0, b0, W1, b1, W2, b2
    d.src_rows = dram("src_rows", [ET * P], FP32)
    d.hi_rows = dram("hi_rows", [ET * P], FP32)
    d.rec = dram("rec", [REC, 2], I32)
    d.marks = dram("marks", [BLK * P * P], U8)
    d.node_max = dram("node_max", [N, C], FP32)
    d.node_sum = dram("node_sum", [N, C], FP32)
    d.x1 = dram("x1", [N + 1, EXT], FP32)
    d.tab = [dram(f"tab{t}", [NPOS + P, C], FP32) for t in range(2)]
    with ExitStack() as keep:
        def sb(name, shape, dt=FP32):
            return keep.enter_context(nc.sbuf_tensor(name, shape, dt))

        k = Names()
        k.ident, k.upper, k.ones = sb("ident", [P, P]), sb("upper", [P, P]), sb("ones", [P, P])
        k.iota = sb("iota", [P, NR], FP16)
        k.D, k.last, k.qsum = sb("D", [NP, NC]), sb("last", [NP, NC]), sb("qsum", [NP, NC])
        ahead = 2 * GT
        k.x_at, k.dst_at = sb("x_at", [P, BLK * P + ahead], U32), sb("dst_at", [P, BLK * P + ahead], U32)
        k.to = sb("to", [P, BLK * P], U32)
        k.last_at, k.w = sb("last_at", [P, NT + ahead], U32), sb("w", [P, NT])
        k.coef, k.eps, k.rounds = sb("coef", [P, 8]), sb("eps", [P, 1]), sb("rounds", [1, 1], I32)
        k.Wd, k.Wb = sb("Wd", [P, P]), sb("Wb", [C + 1, C])
        k.begun = nc.alloc_semaphore("begun")
        count_and_place(nc, d, k)
        with nc.sbuf_tensor("cont", [C, NPOS], U8) as cont:
            k.cont = cont
            read_records(nc, d, k)
            edge_pass(nc, d, k, "M", gather=d.x, scatter=d.node_max, project=True)
            with ExitStack() as scope:
                node_pass(nc, d, k, scope, 0)
                mixing(nc, d, k, scope)
            with nc.sbuf_tensor("Xd", [P, NT, C], FP32) as Xd:
                k.Xd = Xd
                edge_pass(nc, d, k, "H5", gather=d.x1, store=d.tab[0], coef=5)
                for step in (4, 3, 2):
                    edge_pass(nc, d, k, f"H{step}", gather=d.tab[step % 2], store=d.tab[1 - step % 2],
                              coef=step, inner=True)
                edge_pass(nc, d, k, "H1", gather=d.tab[1], scatter=d.node_sum, coef=1)
        with ExitStack() as scope:
            node_pass(nc, d, k, scope, 1)


def count_and_place(nc, d, k):
    with ExitStack() as scope:
        def sb(name, shape, dt=FP32):
            return scope.enter_context(nc.sbuf_tensor(name, shape, dt))

        sem = scope.enter_context(semaphores(nc))
        ids = sb("ids", [P, 2, BLK, P], I32)
        rows = sb("rows", [P, 2, BLK, P])
        hirow = sb("hirow", [P, BLK, P])
        recs = sb("recs", [P, BLK * P, 2])
        hi = sb("hi", [P, 2, BLK * P])
        lo = sb("lo", [P, 2, BLK * P])
        pen = sb("pen", [P, BLK * P])
        mask = sb("mask", [P, GPOS])
        part = sb("part", [P, 2])
        fill = sb("fill", [P, 2, TAB_W])
        rec0 = sb("rec0", [P, 401, 2], I32)
        zrow = sb("zrow", [P, C])
        xpad = sb("xpad", [1, EXT])
        start = sb("start", [NP, NC])

        init = sem("init")
        fills, rec_filled = sem("fills"), sem("rec_filled")
        const_ready, ids_ready, ids_blank = sem("const_ready"), sem("ids_ready"), sem("ids_blank")
        rows_ready, rows_stored = sem("rows_ready"), sem("rows_stored")
        tr_done, tr_free, keys_ready = sem("tr_done"), sem("tr_free"), sem("keys_ready")
        vch, pch = sem("vch"), sem("pch")

        with nc.psum_tensor("tr_ps", [P, 4, BANK], FP32) as tr_ps, nc.Block() as block:
            @block.gpsimd
            def _(pool):
                pool.sem_inc(k.begun, 1)
                link = Chain(pool, pch)
                pool.memset(fill[:, 0, :], NEG).then_inc(init, 1)
                pool.memset(fill[:, 1, :], 0.0).then_inc(init, 1)
                pool.memset(zrow[:], 0.0).then_inc(init, 1)
                link(pool.memset(xpad[:], 0.0))
                pool.memset(xpad[:, C + 1:C + 2], float(ZERO_ROW)).then_inc(init, 1)
                link(pool.memset(k.ident[:], 0.0))
                link(pool.affine_select(out=k.ident[:], in_=k.ident[:], compare_op=ALU.not_equal, fill=1.0,
                                        base=0, pattern=[[-1, P]], channel_multiplier=1))
                link(pool.memset(k.upper[:], 1.0))
                link(pool.affine_select(out=k.upper[:], in_=k.upper[:], compare_op=ALU.is_gt, fill=0.0,
                                        base=0, pattern=[[1, P]], channel_multiplier=-1))
                link(pool.memset(mask[:], 1.0))
                link(pool.affine_select(out=mask[:], in_=mask[:], compare_op=ALU.is_gt, fill=0.0,
                                        base=GPOS - P, pattern=[[-1, GPOS]], channel_multiplier=1))
                pool.iota(part[:], [[-1, 2]], base=0, channel_multiplier=-2, allow_small_or_imprecise_dtypes=True)
                pool.iota(k.iota[:], [[1, NR]], base=0, channel_multiplier=0, allow_small_or_imprecise_dtypes=True)
                pool.memset(k.eps[:], EPS)
                pool.memset(k.ones[:], 1.0).then_inc(const_ready, 1)

            @block.vector
            def _(dve):
                link = Chain(dve, vch)
                dve.memset(ids[:], -1).then_inc(ids_blank, 1)
                link(dve.memset(rec0[:, :, 0], N))
                dve.memset(rec0[:, :, 1], N).then_inc(init, 1)
                dve.wait_ge(ids_ready, 16 * 10)
                link(dve.tensor_copy(rows[:], ids[:]))
                link(dve.tensor_scalar(hirow[:], rows[:, 0], -(NR - 1) / 2, 1.0 / NR, ALU.add, ALU.mult))
                dve.tensor_scalar(hirow[:], hirow[:], ROUND, ROUND, ALU.add, ALU.subtract).then_inc(rows_ready, 1)
                for which in range(2):
                    dve.wait_ge(tr_done, which + 1)
                    link(dve.tensor_copy(recs[:, :, 1 - which], tr_ps[:, which, :]))
                    v, h, l = recs[:, :, 1 - which], hi[:, which], lo[:, which]
                    link(dve.tensor_scalar(h, v, -(NR - 1) / 2, 1.0 / NR, ALU.add, ALU.mult))
                    link(dve.tensor_scalar(h, h, ROUND, ROUND, ALU.add, ALU.subtract))
                    link(dve.scalar_tensor_tensor(l, h, float(-NR), v, ALU.mult, ALU.add))
                link(dve.tensor_scalar(pen[:], recs[:, :, 1], 0.0, FAR, ALU.is_lt, ALU.mult))
                dve.tensor_scalar(pen[:], pen[:], 1.0, None, ALU.add).then_inc(keys_ready, 1)

            @block.tensor
            def _(pe):
                pe.wait_ge(const_ready, 1)
                pe.wait_ge(rows_ready, 1)
                for which in range(2):
                    for b in range(BLK):
                        last = pe.transpose(tr_ps[:, which, b * P:(b + 1) * P], rows[:, which, b, :], k.ident[:])
                    last.then_inc(tr_done, 1)

            @block.sync
            def _(sp):
                sp.wait_ge(ids_blank, 1)
                full = E // P
                for which, v in enumerate((d.src, d.dst)):
                    for b in range(BLK - 1):
                        sp.dma_start(ids[:, which, b, :], v[b * P * P:(b + 1) * P * P].rearrange("(t e) -> t e", e=P)
                                     ).then_inc(ids_ready, 16)
                    t = (BLK - 1) * P
                    sp.dma_start(ids[0:full - t, which, BLK - 1, :], v[t * P:full * P].rearrange("(t e) -> t e", e=P)
                                 ).then_inc(ids_ready, 16)
                    sp.dma_start(ids[full - t:full - t + 1, which, BLK - 1, 0:E - full * P],
                                 v[full * P:E].unsqueeze(0)).then_inc(ids_ready, 16)
                sp.wait_ge(rows_ready, 1)
                for tab, rws in ((d.src_rows, rows[:, 0]), (d.hi_rows, hirow[:, :, :])):
                    for b in range(BLK):
                        n = min(P, ET - b * P)
                        sp.dma_start(tab[b * P * P:(b * P + n) * P].rearrange("(t e) -> t e", e=P), rws[0:n, b, :]
                                     ).then_inc(rows_stored, 16)
                sp.wait_ge(rows_stored, 2 * BLK * 16)

        n_fills = 16 * (2 + 8 + 2 * 2 * (NC * C // NODE_W))

        oh_ready, oh_used = [sem(f"oh_ready{s}") for s in range(2)], [sem(f"oh_used{s}") for s in range(2)]
        zero_ready, counted, cch = sem("zero_ready"), sem("counted"), sem("cch")
        pref_in, pref_out = sem("pref_in"), sem("pref_out")
        with ExitStack() as inner:
            isb = lambda name, shape, dt=FP32: inner.enter_context(nc.sbuf_tensor(name, shape, dt))
            ohp = isb("ohp", [P, 2, 2, NROW], BF16)
            ohc = isb("ohc", [P, 2, 2, NR], BF16)
            zero = isb("zero", [P, BANK], BF16)
            cnt = isb("cnt", [NP, 2, NC])
            inn, cum, part1 = isb("inn", [NP, NC]), isb("cum", [NP, 2, NC]), isb("part1", [NP, 2, NC])
            onesc = isb("onesc", [NP, NC])
            tot = isb("tot", [NP, 2])
            off = isb("off", [NP, 4])
            cps = [inner.enter_context(nc.psum_tensor(f"cps{w}", [NP, 2, BANK], FP32)) for w in range(2)]
            offps = inner.enter_context(nc.psum_tensor("offps", [NP, BANK], FP32))
            block = inner.enter_context(nc.Block())

            @block.vector
            def _(dve):
                dve.memset(zero[:], 0.0).then_inc(zero_ready, 1)
                with dve.Fori(0, ET // 2) as i:
                    for s in range(2):
                        dve.wait_ge(oh_used[s], i)
                        for w in range(2):
                            dve.tensor_scalar(ohp[:, s, w], k.iota[:, 0:NROW], hi[:, w, ds(i * 2 + s, 1)], None,
                                              ALU.is_equal)
                            last = dve.tensor_scalar(ohc[:, s, w], k.iota[:], lo[:, w, ds(i * 2 + s, 1)], None,
                                                     ALU.is_equal)
                        last.then_inc(oh_ready[s], 1)
                link = Chain(dve, cch)
                dve.wait_ge(counted, 1)
                for w in range(2):
                    link(dve.tensor_copy(cnt[:, w].rearrange("p (h c) -> p h c", h=2), cps[w][:, :, 0:NR]))
                link(dve.memset(onesc[:], 1.0))
                hs, hd = cnt[:, 0], cnt[:, 1]
                link(dve.tensor_scalar(inn[:], hd, 0.0, None, ALU.is_gt))
                link(dve.tensor_tensor(part1[:, 0], hs, inn[:], ALU.mult))
                link(dve.tensor_tensor(part1[:, 1], hs, part1[:, 0], ALU.subtract))
                for w in range(2):
                    link(dve.tensor_tensor_scan(cum[:, w], onesc[:], part1[:, w], 0.0, ALU.mult, ALU.add))
                link(dve.tensor_copy(tot[:], cum[:, :, NC - 1]))
                dve.sem_inc(pref_in, 1)
                dve.wait_ge(pref_out, 1)
                link(dve.tensor_copy(off[:], offps[:, 0:4]))
                link(dve.tensor_scalar(off[:, 2:3], off[:, 2:3], 1.0 / (2 * GPOS), 0.5 - 0.5 / (2 * GPOS),
                                       ALU.mult, ALU.add))
                link(dve.tensor_scalar(off[:, 2:3], off[:, 2:3], ROUND, ROUND, ALU.add, ALU.subtract))
                link(dve.tensor_scalar(off[:, 2:3], off[:, 2:3], 1.0, None, ALU.max))
                link(dve.tensor_copy(k.rounds[:], off[0:1, 2:3]))
                link(dve.scalar_tensor_tensor(off[:, 1:2], off[:, 2:3], float(2 * GPOS), off[:, 1:2], ALU.mult, ALU.add))
                for w in range(2):
                    link(dve.scalar_tensor_tensor(cum[:, w], cum[:, w], off[:, w:w + 1], part1[:, w],
                                                  ALU.add, ALU.subtract))
                link(dve.tensor_tensor(cum[:, 0], cum[:, 0], cum[:, 1], ALU.subtract))
                link(dve.tensor_tensor(cum[:, 0], cum[:, 0], inn[:], ALU.mult))
                link(dve.tensor_tensor(start[:], cum[:, 0], cum[:, 1], ALU.add))
                link(dve.tensor_scalar(inn[:], hs, 0.0, None, ALU.is_gt))
                link(dve.scalar_tensor_tensor(k.last[:], start[:], float(-1 - ZERO_ROW), hs, ALU.add, ALU.add))
                link(dve.tensor_tensor(k.last[:], k.last[:], inn[:], ALU.mult))
                link(dve.tensor_scalar(k.last[:], k.last[:], float(ZERO_ROW), None, ALU.add))
                dve.tensor_scalar(k.D[:], hd, 1e-12, None, ALU.max).then_inc(pref_in, 1)
                dve.wait_ge(pref_out, 2)
                link(dve.reciprocal(k.D[:], k.D[:]))

            @block.scalar
            def _(act):
                act.wait_ge(init, 5)
                act.dma_start(d.rec.rearrange("(p t) c -> p t c", p=P), rec0[:]).then_inc(rec_filled, 16)
                act.dma_start(d.x1[N:N + 1, :], xpad[:]).then_inc(fills, 16)
                act.dma_start(d.tab[0][NPOS:NPOS + P, :], zrow[:]).then_inc(fills, 16)
                v = d.tab[1].rearrange("(p r) f -> p (r f)", p=P)
                for c in range(8):
                    act.dma_start(v[:, c * TAB_W:(c + 1) * TAB_W], fill[:, 1, :]).then_inc(fills, 16)
                for t, tab in enumerate((d.node_max, d.node_sum)):
                    v = tab.rearrange("(p c) f -> p (c f)", c=NC)
                    w = NODE_W
                    for c in range(NC * C // w):
                        for a, b in zip(SPLIT, SPLIT[1:]):
                            act.dma_start(v[a:b, c * w:(c + 1) * w], fill[a:b, t, 0:NODE_W]).then_inc(fills, 16)
                act.wait_ge(pref_in, 2)
                act.activation(k.D[:], k.D[:], ACT.Sqrt).then_inc(pref_out, 1)

            @block.tensor
            def _(pe):
                pe.wait_ge(zero_ready, 1)
                for w in range(2):
                    for h in range(2):
                        pe.matmul(cps[w][:, h, 0:NR], zero[:, 0:NP], zero[:, 0:NR], start=True, stop=True)
                with pe.Fori(0, ET // 2) as i:
                    for s in range(2):
                        pe.wait_ge(oh_ready[s], i + 1)
                        for w in range(2):
                            for h in range(2):
                                last = pe.matmul(cps[w][:, h, 0:NR], ohp[:, s, w, h::2], ohc[:, s, w],
                                                 start=False, stop=True, skip_group_check=True)
                        last.then_inc(oh_used[s], 1)
                for s in range(2):
                    pe.wait_ge(oh_used[s], ET // 2)
                pe.sem_inc(counted, 1)
                pe.wait_ge(pref_in, 1)
                pe.matmul(offps[:, 0:2], k.upper[0:NP, 0:NP], tot[:], start=True, stop=True)
                pe.matmul(offps[:, 2:4], k.ones[0:NP, 0:NP], tot[:], start=True, stop=True).then_inc(pref_out, 1)

        two = lambda name: [sem(f"{name}{s}") for s in range(2)]
        rows_in, rows_used, dist_done, hiT_ready = two("rows_in"), two("rows_used"), two("dist_done"), two("hiT_ready")
        onehots, added, table_ready = two("onehots"), two("added"), two("table_ready")
        got, got_read, pos_ready = two("got"), two("got_read"), two("pos_ready")
        rec_ready, scattered, summed = two("rec_ready"), two("scattered"), two("summed")
        seeded = sem("seeded")
        with ExitStack() as inner:
            isb = lambda name, shape, dt=FP32: inner.enter_context(nc.sbuf_tensor(name, shape, dt))
            hibc, srcbc = isb("hibc", [P, 2, GPOS]), isb("srcbc", [P, 2, GPOS])
            dist = isb("dist", [NP, 2, GPOS])
            hiT = isb("hiT", [NP, 2, 2, GPOS])
            ohp = isb("ohp2", [P, 2, 4, NROW], BF16)
            ohc = isb("ohc2", [P, 2, 4, NR], BF16)
            table = isb("table", [NP, 2, 2, NR])
            eq = isb("eq", [P, 4, GPOS], BF16)
            picked = isb("picked", [P, 4, NR], BF16)
            at, rank = isb("at", [P, 2, 4]), isb("rank", [P, 2, 4])
            pos = isb("pos", [P, 2, 4], U32)
            rec = isb("rec_sb", [P, 2, 4, 2], I32)
            tps = inner.enter_context(nc.psum_tensor("tps", [NP, 2, BANK], FP32))
            gps = [inner.enter_context(nc.psum_tensor(f"gps{s}", [P, BANK], FP32)) for s in range(2)]
            block = inner.enter_context(nc.Block())
            LAST = EB // 2 - 1

            @block.sync
            def _(sp):
                with sp.Fori(0, EB // 2) as i:
                    for s in range(2):
                        before, twice = settle(sp, k, i, i * 2)
                        sp.wait_ge(rows_used[s], before)
                        sp.wait_ge(dist_done[s], twice)
                        for to, of in ((hibc, d.hi_rows), (srcbc, d.src_rows)):
                            sp.dma_start(to[:, s], of[ds(i * (2 * GPOS) + s * GPOS, GPOS)].partition_broadcast(P)
                                         ).then_inc(rows_in[s], 16)

            @block.vector
            def _(dve):
                def prepare(i, s):
                    dve.wait_ge(added[s], i)
                    for j in range(4):
                        t = ds(i * 8 + s * 4 + j, 1)
                        dve.tensor_scalar(ohp[:, s, j], k.iota[:, 0:NROW], hi[:, 0, t], None, ALU.is_equal)
                        last = dve.tensor_scalar(ohc[:, s, j], k.iota[:], lo[:, 0, t], None, ALU.is_equal)
                    last.then_inc(onehots[s], 1)
                    dve.wait_ge(rows_in[s], i * 32 + 32)
                    for j in range(4):
                        t, n = ds(i * 8 + s * 4 + j, 1), (j + 1) * P
                        last = dve.scalar_tensor_tensor(eq[:, j, 0:n], srcbc[:, s, 0:n], recs[:, t, 1],
                                                        mask[:, GPOS - n:GPOS], ALU.is_equal, ALU.mult,
                                                        accum_out=rank[:, s, j:j + 1])
                    last.then_inc(rows_used[s], 1)
                    dve.wait_ge(rows_used[s], i + 1)

                def place(i, s):
                    dve.wait_ge(onehots[s], i + 1)
                    for j in range(4):
                        dve.wait_ge(got[j % 2], i * 4 + 2 * s + j // 2 + 1)
                        dve.scalar_tensor_tensor(picked[:, j], gps[j % 2][:, 0:NR], 1.0, ohc[:, s, j],
                                                 ALU.mult, ALU.mult, accum_out=at[:, s, j:j + 1]
                                                 ).then_inc(got_read[j % 2], 1)
                    for r in range(2):
                        dve.wait_ge(got_read[r], i * 4 + 2 * s + 2)
                    dve.tensor_tensor(at[:, s], at[:, s], rank[:, s], ALU.add).then_inc(summed[s], 1)
                    dve.wait_ge(summed[s], i + 1)
                    dve.wait_ge(scattered[s], i * 64)
                    dve.tensor_tensor(pos[:, s], at[:, s], pen[:, ds(i * 8 + s * 4, 4)], ALU.add
                                      ).then_inc(pos_ready[s], 1)

                prepare(0, 0)
                with dve.Fori(0, LAST) as i:
                    prepare(i, 1)
                    place(i, 0)
                    prepare(i + 1, 0)
                    place(i, 1)
                prepare(LAST, 1)
                place(LAST, 0)
                place(LAST, 1)

            @block.tensor
            def _(pe):
                for h in range(2):
                    last = pe.matmul(tps[:, h, 0:NR], k.ident[0:NP, 0:NP], start[:, h * NR:(h + 1) * NR],
                                     start=True, stop=True)
                last.then_inc(seeded, 1)
                with pe.Fori(0, EB // 2) as i:
                    for s in range(2):
                        pe.wait_ge(hiT_ready[s], i + 1)
                        pe.wait_ge(table_ready[s], i + 1)
                        for j in range(4):
                            pe.wait_ge(got_read[j % 2], i * 4 + 2 * s + j // 2)
                            for h in range(2):
                                last = pe.matmul(gps[j % 2][:, 0:NR], hiT[:, s, h, j * P:(j + 1) * P], table[:, s, h],
                                                 start=h == 0, stop=h == 1)
                            last.then_inc(got[j % 2], 1)
                        pe.wait_ge(onehots[s], i + 1)
                        for j in range(4):
                            for h in range(2):
                                last = pe.matmul(tps[:, h, 0:NR], ohp[:, s, j, h::2], ohc[:, s, j],
                                                 start=False, stop=True, skip_group_check=True)
                        last.then_inc(added[s], 1)

            @block.scalar
            def _(act):
                def rows(i, s):
                    act.wait_ge(rows_in[s], i * 32 + 32)
                    act.wait_ge(hiT_ready[1 - s], i + s)
                    for h in range(2):
                        act.activation(dist[:, h], hibc[0:NP, s], ACT.Abs, bias=part[0:NP, h:h + 1]
                                       ).then_inc(dist_done[s], 1)
                    act.wait_ge(dist_done[s], i * 2 + 2)
                    act.wait_ge(added[s], i)
                    act.activation(hiT[:, s], dist[:], ACT.Relu, bias=1.0, scale=-1.0).then_inc(hiT_ready[s], 1)

                def records(i, s):
                    act.wait_ge(scattered[s], i * 64)
                    act.activation(rec[:, s], recs[:, ds(i * 8 + s * 4, 4), :], ACT.Copy).then_inc(rec_ready[s], 1)

                def snapshot(i, s):
                    act.wait_ge(added[s], i + 1)
                    act.activation(table[:, 1 - s], tps[:, :, 0:NR], ACT.Copy).then_inc(table_ready[1 - s], 1)

                rows(0, 0)
                act.wait_ge(seeded, 1)
                act.activation(table[:, 0], tps[:, :, 0:NR], ACT.Copy).then_inc(table_ready[0], 1)
                with act.Fori(0, LAST) as i:
                    records(i, 0)
                    rows(i, 1)
                    snapshot(i, 0)
                    records(i, 1)
                    rows(i + 1, 0)
                    snapshot(i, 1)
                records(LAST, 0)
                rows(LAST, 1)
                snapshot(LAST, 0)
                records(LAST, 1)
                act.wait_ge(fills, n_fills)

            @block.gpsimd
            def _(pool):
                pool.wait_ge(rec_filled, 16)
                with pool.Fori(0, EB // 2) as i:
                    for s in range(2):
                        again, = settle(pool, k, i + 1)
                        pool.wait_ge(pos_ready[s], again)
                        pool.wait_ge(rec_ready[s], again)
                        for j in range(4):
                            pool.indirect_dma_start(
                                out=d.rec, out_offset=bass.IndirectOffsetOnAxis(ap=pos[:, s, j:j + 1], axis=0),
                                in_=rec[:, s, j, :], in_offset=None, bounds_check=REC - 1, oob_is_err=False,
                            ).then_inc(scattered[s], 16)
                for s in range(2):
                    pool.wait_ge(scattered[s], EB // 2 * 64)


def read_records(nc, d, k):
    with ExitStack() as scope:
        def sb(name, shape, dt=FP32):
            return scope.enter_context(nc.sbuf_tensor(name, shape, dt))

        sem = scope.enter_context(semaphores(nc))
        raw = sb("raw", [P, 3, BLK, P, 2], I32)
        same = sb("same", [P, BLK, P], U8)
        val = sb("val", [P, 2, BLK, P])
        tmp = sb("tmp", [P, BLK, P])
        ps = [scope.enter_context(nc.psum_tensor(f"idx_ps{w}", [P, BANK], FP32)) for w in range(2)]
        loaded, blank, marked, stored, bcast = sem("loaded"), sem("blank"), sem("marked"), sem("stored"), sem("bcast")
        vch, tr_in, tr_out = sem("vch3"), sem("tr_in3"), sem("tr_out3")
        wa, wb = sb("wa", [P, C]), sb("wb", [P, C])
        weights_in, pch = sem("weights_in"), sem("pch3")
        block = scope.enter_context(nc.Block())

        @block.sync
        def _(sp):
            sp.wait_ge(blank, 1)
            for shift in range(3):
                for b in range(BLK):
                    n = min(P, NT - b * P)
                    at = b * P * P + shift
                    sp.dma_start(raw[0:n, shift, b], d.rec[at:at + n * P, :].rearrange("(t p) c -> t p c", p=P)
                                 ).then_inc(loaded, 16)
            sp.wait_ge(marked, 1)
            sp.dma_start(d.marks.rearrange("(b t p) -> t b p", t=P, p=P), same[:]).then_inc(stored, 16)
            sp.wait_ge(stored, 16)
            q = NPOS // 4
            for c in range(4):
                sp.dma_start(k.cont[:, c * q:(c + 1) * q], d.marks[c * q:(c + 1) * q].partition_broadcast(C)
                             ).then_inc(bcast, 16)
            sp.wait_ge(bcast, 64)

        @block.vector
        def _(dve):
            link = Chain(dve, vch)
            dve.memset(raw[:], 0).then_inc(blank, 1)
            dve.memset(k.dst_at[:, BLK * P:], 0)
            dve.memset(k.x_at[:, BLK * P:], 0)
            dve.memset(k.last_at[:, NT:], 0)
            dve.wait_ge(loaded, 3 * BLK * 16)
            dve.tensor_tensor(same[:], raw[:, 1, :, :, 1], raw[:, 0, :, :, 1], ALU.is_equal).then_inc(marked, 1)
            link(dve.tensor_copy(val[:, 0], raw[:, 1, :, :, 0]))
            link(dve.tensor_tensor(tmp[:], raw[:, 1, :, :, 1], raw[:, 2, :, :, 1], ALU.is_equal))
            dve.scalar_tensor_tensor(val[:, 1], tmp[:], FAR, raw[:, 1, :, :, 1], ALU.mult, ALU.add).then_inc(tr_in, 1)
            dve.wait_ge(tr_out, 1)
            dve.tensor_copy(k.dst_at[:, 0:BLK * P], ps[0][:])
            dve.tensor_scalar(k.x_at[:, 0:BLK * P], ps[0][:], float(N - 1), None, ALU.min)
            link(dve.tensor_copy(k.to[:, 0:BLK * P], ps[1][:]))

        @block.tensor
        def _(pe):
            pe.wait_ge(tr_in, 1)
            for w in range(2):
                for b in range(BLK):
                    last = pe.transpose(ps[w][:, b * P:(b + 1) * P], val[:, w, b, :], k.ident[:])
            last.then_inc(tr_out, 1)

        @block.scalar
        def _(act):
            act.dma_start(k.Wb[0:C, :], d.W0[C:2 * C, :]).then_inc(weights_in, 16)
            act.dma_start(k.Wb[C:C + 1, :], d.b0.unsqueeze(0)).then_inc(weights_in, 16)
            for h in range(2):
                act.dma_start(wa[h * C:(h + 1) * C, :], d.W0[0:C, :]).then_inc(weights_in, 16)
                act.dma_start(wb[h * C:(h + 1) * C, :], d.W0[C:2 * C, :]).then_inc(weights_in, 16)
            act.wait_ge(weights_in, 6 * 16)

        @block.gpsimd
        def _(pool):
            link = Chain(pool, pch)
            link(pool.memset(k.Wd[:], 0.0))
            pool.wait_ge(weights_in, 6 * 16)
            for h in range(2):
                a, b = h * C, (h + 1) * C
                link(pool.tensor_tensor(k.Wd[a:b, a:b], wa[a:b, :], wb[a:b, :], ALU.subtract))


def edge_pass(nc, d, k, name, gather, store=None, scatter=None, project=False, coef=None, inner=False):
    first = coef == 5
    width = EXT if first else C
    with ExitStack() as scope:
        def sb(nm, shape, dt=FP32):
            return scope.enter_context(nc.sbuf_tensor(f"{nm}_{name}", shape, dt))

        def ps(nm, shape):
            return [scope.enter_context(nc.psum_tensor(f"{nm}{s}_{name}", shape, FP32)) for s in range(2)]

        sem = scope.enter_context(semaphores(nc))

        def two(nm):
            return [sem(f"{nm}{s}_{name}") for s in range(2)]

        at = sb("at", [P, 2, GT], U32)
        to = sb("to", [P, 2, GT], U32) if scatter is not None else None
        rows = sb("rows", [P, 2, GT, width])
        own = sb("own", [P, 2, GT, C]) if not project and not first else None
        z = sb("z", [P, 2, GT, C]) if not project else rows
        sums = sb("sums", [C, 2, GPOS])
        back = sb("back", [P, 2, GT, C])
        zT = ps("zT", [C, BANK])
        backT = ps("backT", [P, BANK])
        if project:
            xT = sb("xT", [C + 1, 2, GPOS])
            pen = sb("pen", [C, 2, GPOS])
            vT = ps("vT", [C, BANK])
            xT_ready, pen_ready, vT_done = two("xT_ready"), two("pen_ready"), two("vT_done")
        at_ready, gathered = two("at_ready"), two("gathered")
        own_ready, z_ready, zT_done = two("own_ready"), two("z_ready"), two("zT_done")
        scanned, backT_done, back_ready = two("scanned"), two("backT_done"), two("back_ready")
        away = two("away")
        begun, ich = (sem(f"{nm}_{name}") for nm in ("begun", "ich"))
        at_table = k.x_at if project else k.dst_at if first else k.last_at

        block = scope.enter_context(nc.Block())

        def rounds(eng):
            return eng.value_load(k.rounds[0:1, 0:1], min_val=1, max_val=NG // 2) if inner else NG // 2

        @block.gpsimd
        def _(pool):
            def gather_group(i, s):
                again, = settle(pool, k, i + 1)
                pool.wait_ge(at_ready[s], again)
                pool.wait_ge((zT_done if project else z_ready)[s], i)
                for j in range(GT):
                    pool.indirect_dma_start(
                        out=rows[:, s, j, :], out_offset=None, in_=gather,
                        in_offset=bass.IndirectOffsetOnAxis(ap=at[:, s, j:j + 1], axis=0),
                    ).then_inc(gathered[s], 16)

            def scatter_group(i, s):
                again, = settle(pool, k, i + 1)
                pool.wait_ge(back_ready[s], again)
                for j in range(GT):
                    pool.indirect_dma_start(
                        out=scatter, out_offset=bass.IndirectOffsetOnAxis(ap=to[:, s, j:j + 1], axis=0),
                        in_=back[:, s, j, :], in_offset=None, bounds_check=N - 1, oob_is_err=False,
                    ).then_inc(away[s], 16)

            if scatter is None:
                with pool.Fori(0, rounds(pool)) as i:
                    for s in range(2):
                        gather_group(i, s)
            else:
                for s in range(2):
                    gather_group(0, s)
                with pool.Fori(1, NG // 2) as i:
                    for s in range(2):
                        gather_group(i, s)
                        scatter_group(i - 1, s)
                for s in range(2):
                    scatter_group(NG // 2 - 1, s)
                for s in range(2):
                    pool.wait_ge(away[s], NG // 2 * GT * 16)

        @block.sync
        def _(sp):
            if store is not None:
                n = rounds(sp)
                with sp.Fori(0, n) as i:
                    for s in range(2):
                        sp.wait_ge(back_ready[s], i + 1)
                        sp.dma_start(store[ds(i * (2 * GPOS) + s * GPOS, GPOS), :].rearrange("(j p) f -> p j f", p=P),
                                     back[:, s]).then_inc(away[s], 16)
                landed, = settle(sp, k, n * 16)
                for s in range(2):
                    sp.wait_ge(away[s], landed)

        @block.scalar
        def _(act):
            def fetch(i, s):
                act.wait_ge(gathered[s], i * (GT * 16))
                act.activation(at[:, s], at_table[:, ds(i * (2 * GT) + s * GT, GT)], ACT.Copy
                               ).then_inc(at_ready[s], 1)

            def prepare(i, s):
                if project:
                    act.wait_ge(scanned[s], i)
                    act.activation(pen[:, s], k.cont[:, ds(i * (2 * GPOS) + s * GPOS, GPOS)], ACT.Copy,
                                   bias=NEG, scale=-NEG).then_inc(pen_ready[s], 1)
                elif not first:
                    act.wait_ge(z_ready[s], i)
                    act.activation(own[:, s], k.Xd[:, ds(i * (2 * GT) + s * GT, GT), :], ACT.Copy,
                                   scale=k.coef[:, coef:coef + 1]).then_inc(own_ready[s], 1)

            def group(i, s):
                if project:
                    act.wait_ge(zT_done[s], i + 1)
                    act.wait_ge(vT_done[s], i)
                    act.activation(xT[0:C, s], zT[s][:], ACT.Copy).then_inc(xT_ready[s], 1)
                act.wait_ge(backT_done[s], i + 1)
                act.wait_ge(away[s], i * (16 if scatter is None else 16 * GT))
                if scatter is not None:
                    act.activation(to[:, s], k.to[:, ds(i * (2 * GT) + s * GT, GT)], ACT.Copy)
                act.activation(back[:, s].rearrange("p j c -> p (j c)"), backT[s][:, 0:GT * C], ACT.Copy
                               ).then_inc(back_ready[s], 1)

            n = rounds(act)
            for s in range(2):
                fetch(0, s)
            with act.Fori(0, n) as i:
                prepare(i, 0)
                fetch(i + 1, 0)
                prepare(i, 1)
                group(i, 0)
                fetch(i + 1, 1)
                group(i, 1)

        @block.vector
        def _(dve):
            n = rounds(dve)
            if project:
                dve.memset(xT[C:C + 1, :, :], 1.0).then_inc(begun, 1)
            dve.memset(sums[:, 1, GPOS - 1:GPOS], 0.0).then_inc(ich, 1)
            dve.wait_ge(ich, 1)
            with dve.Fori(0, n) as i:
                for s in range(2):
                    if not project:
                        dve.wait_ge(gathered[s], i * (GT * 16) + GT * 16)
                        dve.wait_ge(zT_done[s], i)
                        tiles = ds(i * (2 * GT) + s * GT, GT)
                    if first:
                        last_D = rows[:, s, :, C]
                        dve.tensor_copy(k.last_at[:, tiles], rows[:, s, :, C + 1])
                        dve.tensor_tensor(k.w[:, tiles], last_D, last_D, ALU.mult)
                        for j in range(GT):
                            D = rows[:, s, j, C:C + 1]
                            dve.tensor_scalar(k.Xd[:, ds(i * (2 * GT) + s * GT + j, 1), :].rearrange("p a c -> p (a c)"),
                                              rows[:, s, j, 0:C], D, None, ALU.mult)
                            last = dve.tensor_scalar(z[:, s, j], rows[:, s, j, 0:C], D, k.coef[:, 5:6],
                                                     ALU.mult, ALU.mult)
                        last.then_inc(z_ready[s], 1)
                    elif not project:
                        dve.wait_ge(own_ready[s], i + 1)
                        for j in range(GT):
                            last = dve.scalar_tensor_tensor(z[:, s, j], rows[:, s, j],
                                                            k.w[:, ds(i * (2 * GT) + s * GT + j, 1)],
                                                            own[:, s, j], ALU.mult, ALU.add)
                        last.then_inc(z_ready[s], 1)
                    dve.wait_ge((vT_done if project else zT_done)[s], i + 1)
                    dve.wait_ge(backT_done[s], i)
                    dve.wait_ge(scanned[1 - s], i + s)
                    state = sums[:, 1 - s, GPOS - 1:GPOS]
                    if project:
                        dve.wait_ge(pen_ready[s], i + 1)
                        dve.tensor_tensor_scan(sums[:, s], pen[:, s], vT[s][:], state, ALU.add, ALU.max
                                               ).then_inc(scanned[s], 1)
                    else:
                        cont = k.cont[:, ds(i * (2 * GPOS) + s * GPOS, GPOS)]
                        dve.tensor_tensor_scan(sums[:, s], cont, zT[s][:], state, ALU.mult, ALU.add
                                               ).then_inc(scanned[s], 1)

        @block.tensor
        def _(pe):
            n = rounds(pe)
            if project:
                pe.wait_ge(begun, 1)
            with pe.Fori(0, n) as i:
                for s in range(2):
                    again, rows_in = settle(pe, k, i + 1, i * (GT * 16) + GT * 16)
                    if project:
                        pe.wait_ge(gathered[s], rows_in)
                        pe.wait_ge(xT_ready[s], i)
                    else:
                        pe.wait_ge(z_ready[s], again)
                        pe.wait_ge(scanned[s], i)
                    for j in range(GT):
                        last = pe.transpose(zT[s][:, j * P:(j + 1) * P], z[:, s, j, 0:C], k.ident[:])
                    last.then_inc(zT_done[s], 1)
                    if project:
                        pe.wait_ge(xT_ready[s], i + 1)
                        pe.wait_ge(scanned[s], i)
                        pe.matmul(vT[s][:], k.Wb[:], xT[:, s], start=True, stop=True).then_inc(vT_done[s], 1)
                    settle(pe, k)
                    pe.wait_ge(scanned[s], again)
                    pe.wait_ge(back_ready[s], i)
                    for j in range(GT):
                        last = pe.transpose(backT[s][:, j * C:(j + 1) * C], sums[:, s, j * P:(j + 1) * P],
                                            k.ident[0:C, 0:C])
                    last.then_inc(backT_done[s], 1)


def node_pass(nc, d, k, scope, layer):
    def sb(nm, shape, dt=FP32):
        return scope.enter_context(nc.sbuf_tensor(f"{nm}_n{layer}", shape, dt))

    def ps(nm, shape):
        return scope.enter_context(nc.psum_tensor(f"{nm}_n{layer}", shape, FP32))

    wide = EXT if layer else C
    xin = sb("xin", [NP, 2, KN, wide])
    agg = sb("agg", [NP, 2, KN, C])
    pre, y, cent, sq = (sb(nm, [NP, 2, KN, C]) for nm in ("pre", "y", "cent", "sq"))
    res = sb("res", [NP, 2, KN, C if layer else EXT])
    mean, ssq, std, rstd = (sb(nm, [NP, 2, KN]) for nm in ("mean", "ssq", "std", "rstd"))
    table = (d.x1[0:N, :] if layer else d.x).rearrange("(p c) f -> p c f", c=NC)
    edges = (d.node_sum if layer else d.node_max).rearrange("(p c) f -> p c f", c=NC)
    target = (d.out if layer else d.x1[0:N, :]).rearrange("(p c) f -> p c f", c=NC)
    if not layer:
        xT = sb("xT", [P, 2, KN // 2, P])
        xTp = ps("xTp", [P, KN // 2, P])
        ap = [ps(f"ap{s}", [NP, KN, C]) for s in range(2)]
        k.sums_ps = ps("sums", [1, BANK])
        zero = sb("zero", [P, BANK], BF16)

    with ExitStack() as sems:
        sem = sems.enter_context(semaphores(nc))

        def two(nm):
            return [sem(f"{nm}{s}_n{layer}") for s in range(2)]

        loaded, pre_done, y_done, mean_done, cent_done = (two(x) for x in ("loaded", "pre_done", "y_done", "mean_done", "cent_done"))
        sq_done, ssq_done, std_done, rstd_done, res_done = (two(x) for x in ("sq_done", "ssq_done", "std_done", "rstd_done", "res_done"))
        stored, xT_done, xT_ready, a_done, summed, side = (two(x) for x in ("stored", "xT_done", "xT_ready", "a_done", "summed", "side"))
        zeroed, vch, squared = (sem(f"{nm}_n{layer}") for nm in ("zeroed", "vch", "squared"))
        block = sems.enter_context(nc.Block())

        LAST = NCH // 2 - 1

        def staggered(eng, front, tail):
            front(0, 0)
            with eng.Fori(0, LAST) as i:
                front(i, 1)
                tail(i, 0)
                front(i + 1, 0)
                tail(i, 1)
            front(LAST, 1)
            tail(LAST, 0)
            tail(LAST, 1)

        @block.gpsimd
        def _(pool):
            def centre(i, s):
                pool.wait_ge(mean_done[s], i + 1)
                pool.wait_ge(res_done[s], i)
                pool.wait_ge(sq_done[s], i)
                pool.tensor_tensor(cent[:, s], y[:, s], bc(mean[:, s], C), ALU.subtract).then_inc(cent_done[s], 1)

            def scale(i, s):
                pool.wait_ge(cent_done[s], i + 1)
                pool.wait_ge(rstd_done[s], i + 1)
                pool.wait_ge(stored[s], i * 32)
                if not layer:
                    pool.wait_ge(summed[s], i)
                pool.tensor_tensor(res[:, s, :, 0:C], cent[:, s], bc(rstd[:, s], C), ALU.mult).then_inc(res_done[s], 1)

            staggered(pool, centre, scale)

        @block.sync
        def _(sp):
            def load(i, s):
                cols = ds(i * (2 * KN) + s * KN, KN)
                sp.wait_ge(y_done[s], i)
                if not layer:
                    sp.wait_ge(xT_done[s], i)
                node_dma(sp, loaded[s], lambda a, b: xin[a:b, s], lambda a, b: table[a:b, cols, :])
                node_dma(sp, loaded[s], lambda a, b: agg[a:b, s], lambda a, b: edges[a:b, cols, :])

            with sp.Fori(0, NCH // 2) as i:
                for s in range(2):
                    load(i, s)

        @block.scalar
        def _(act):
            def turn(i, s):
                act.wait_ge(xT_done[s], i + 1)
                act.wait_ge(a_done[s], i)
                act.activation(xT[:, s, :, 0:NP], xTp[:, :, 0:NP], ACT.Copy).then_inc(xT_ready[s], 1)

            def front(i, s):
                if not layer:
                    if isinstance(i, int) and i == s == 0:
                        turn(0, 0)
                    act.wait_ge(stored[s], i * 32)
                    cols = ds(i * (2 * KN) + s * KN, KN)
                    act.activation(res[:, s, :, C], k.D[:, cols], ACT.Copy)
                    act.activation(res[:, s, :, C + 1], k.last[:, cols], ACT.Copy).then_inc(side[s], 1)
                    if s == 0:
                        turn(i, 1)
                    elif not (isinstance(i, int) and i == LAST):
                        turn(i + 1, 0)
                act.wait_ge(cent_done[s], i + 1)
                act.wait_ge(ssq_done[s], i)
                act.activation(sq[:, s], cent[:, s], ACT.Square).then_inc(sq_done[s], 1)

            def tail(i, s):
                act.wait_ge(ssq_done[s], i + 1)
                act.wait_ge(rstd_done[s], i)
                act.activation(std[:, s], ssq[:, s], ACT.Sqrt, bias=k.eps[0:NP, :], scale=1.0 / C
                               ).then_inc(std_done[s], 1)
                act.wait_ge(res_done[s], i + 1)
                cols = ds(i * (2 * KN) + s * KN, KN)
                node_dma(act, stored[s], lambda a, b: target[a:b, cols, :], lambda a, b: res[a:b, s])

            staggered(act, front, tail)
            for s in range(2):
                act.wait_ge(stored[s], NCH // 2 * 32)

        @block.vector
        def _(dve):
            if not layer:
                dve.memset(zero[:], 0.0).then_inc(zeroed, 1)

            def front(i, s):
                cols = ds(i * (2 * KN) + s * KN, KN)
                dve.wait_ge(loaded[s], i * 64 + 64)
                dve.wait_ge(cent_done[s], i)
                if layer:
                    dve.tensor_tensor(pre[:, s], agg[:, s], bc(k.D[:, cols], C), ALU.mult).then_inc(pre_done[s], 1)
                    dve.wait_ge(pre_done[s], i + 1)
                    dve.scalar_tensor_tensor(y[:, s], xin[:, s, :, 0:C], k.coef[0:NP, 6:7], pre[:, s],
                                             ALU.mult, ALU.add).then_inc(y_done[s], 1)
                else:
                    dve.wait_ge(a_done[s], i + 1)
                    dve.tensor_tensor(pre[:, s], ap[s][:], agg[:, s], ALU.add).then_inc(pre_done[s], 1)
                    dve.wait_ge(pre_done[s], i + 1)
                    dve.scalar_tensor_tensor(y[:, s], pre[:, s], 0.0, xin[:, s], ALU.max, ALU.add
                                             ).then_inc(y_done[s], 1)
                dve.wait_ge(y_done[s], i + 1)
                dve.tensor_reduce(mean[:, s], y[:, s], AX.X, ALU.add).then_inc(vch, 1)
                dve.wait_ge(vch, i * 2 + s + 1)
                dve.tensor_scalar(mean[:, s], mean[:, s], 1.0 / C, None, ALU.mult).then_inc(mean_done[s], 1)

            def tail(i, s):
                dve.wait_ge(sq_done[s], i + 1)
                dve.wait_ge(std_done[s], i)
                dve.tensor_reduce(ssq[:, s], sq[:, s], AX.X, ALU.add).then_inc(ssq_done[s], 1)
                dve.wait_ge(std_done[s], i + 1)
                dve.wait_ge(res_done[s], i)
                dve.reciprocal(rstd[:, s], std[:, s]).then_inc(rstd_done[s], 1)
                if not layer:
                    q = k.qsum[:, ds(i * (2 * KN) + s * KN, KN)]
                    dve.wait_ge(rstd_done[s], i + 1)
                    dve.scalar_tensor_tensor(q, rstd[:, s], 1.0, rstd[:, s], ALU.mult, ALU.mult).then_inc(squared, 1)
                    dve.wait_ge(squared, i * 2 + s + 1)
                    dve.tensor_tensor(q, q, ssq[:, s], ALU.mult)

            staggered(dve, front, tail)

        if not layer:
            @block.tensor
            def _(pe):
                pe.wait_ge(zeroed, 1)
                pe.matmul(k.sums_ps[:], zero[:, 0:1], zero[:], start=True, stop=True)

                def front(i, s):
                    pe.wait_ge(loaded[s], i * 64 + 64)
                    pe.wait_ge(xT_ready[1 - s], i + s)
                    for j in range(KN // 2):
                        last = pe.transpose(xTp[:, j, 0:NP], xin[:, s, 2 * j:2 * j + 2, :].rearrange("p a c -> p (a c)"),
                                            k.ident[0:NP, 0:NP])
                    last.then_inc(xT_done[s], 1)
                    pe.wait_ge(xT_ready[s], i + 1)
                    pe.wait_ge(pre_done[s], i)
                    for j in range(KN // 2):
                        last = pe.matmul(ap[s][:, 2 * j:2 * j + 2, :], xT[:, s, j, 0:NP], k.Wd[:], start=True, stop=True)
                    last.then_inc(a_done[s], 1)

                def tail(i, s):
                    pe.wait_ge(res_done[s], i + 1)
                    for h in range(KN // 8):
                        last = pe.matmul(k.sums_ps[:], k.ones[0:NP, 0:1], res[:, s, 8 * h:8 * h + 8, 0:C],
                                         start=False, stop=True, skip_group_check=True)
                    last.then_inc(summed[s], 1)

                front(0, 0)
                front(0, 1)
                with pe.Fori(0, LAST) as i:
                    for s in range(2):
                        front(i + 1, s)
                        tail(i, s)
                for s in range(2):
                    tail(LAST, s)


def mixing(nc, d, k, scope):
    def sb(nm, shape):
        return scope.enter_context(nc.sbuf_tensor(nm, shape, FP32))

    F = C + 4
    part, csum, feat = sb("c_part", [1, BANK]), sb("c_sum", [1, C]), sb("c_feat", [1, F])
    qs, tiny = sb("c_q", [NP, 1]), sb("c_tiny", [1, 8])
    w1, b1, prod, h = sb("c_w1", [HID, F]), sb("c_b1", [HID, 1]), sb("c_prod", [HID, F]), sb("c_h", [HID, 2])
    w2, b2, lg, cf = sb("c_w2", [HID, NCOEF]), sb("c_b2", [1, NCOEF]), sb("c_lg", [1, 8]), sb("c_cf", [1, 8])
    with ExitStack() as own:
        sem = own.enter_context(semaphores(nc))
        w_in, vch, to_pe, of_pe, to_act, of_act = (sem(x) for x in ("c_w_in", "c_vch", "c_to_pe", "c_of_pe", "c_to_act", "c_of_act"))
        cps = own.enter_context(nc.psum_tensor("c_ps", [P, BANK], FP32))
        block = own.enter_context(nc.Block())
        total = float(N * C)

        @block.sync
        def _(sp):
            sp.dma_start(w1[:], d.W1).then_inc(w_in, 16)
            sp.dma_start(b1[:], d.b1.unsqueeze(1)).then_inc(w_in, 16)
            sp.dma_start(b2[:], d.b2.unsqueeze(0)).then_inc(w_in, 16)
            with nc.allow_non_contiguous_dma(reason="192 weights, turned"):
                sp.dma_start(w2[:], d.W2.rearrange("k h -> h k")).then_inc(w_in, 16)

        @block.vector
        def _(dve):
            link = Chain(dve, vch)
            link(dve.tensor_copy(part[:], k.sums_ps[:]))
            link(dve.tensor_reduce(csum[:], part[:].rearrange("p (a c) -> p c a", c=C), AX.X, ALU.add))
            link(dve.tensor_scalar(feat[:, 0:C], csum[:], 1.0 / N, None, ALU.mult))
            link(dve.tensor_reduce(tiny[:, 0:1], csum[:], AX.X, ALU.add))
            link(dve.tensor_scalar(feat[:, C:C + 1], tiny[:, 0:1], 1.0 / total, None, ALU.mult))
            dve.tensor_reduce(qs[:], k.qsum[:], AX.X, ALU.add).then_inc(to_pe, 1)
            dve.wait_ge(of_pe, 1)
            link(dve.tensor_tensor(tiny[:, 1:2], feat[:, C:C + 1], tiny[:, 0:1], ALU.mult))
            link(dve.tensor_tensor(tiny[:, 2:3], cps[0:1, 0:1], tiny[:, 1:2], ALU.subtract))
            dve.tensor_scalar(tiny[:, 3:4], tiny[:, 2:3], 1.0 / (total - 1), None, ALU.mult).then_inc(to_act, 1)
            dve.memset(feat[:, C + 2:C + 3], float(N))
            link(dve.memset(feat[:, C + 3:C + 4], float(E)))
            dve.wait_ge(of_act, 1)
            dve.sem_inc(to_pe, 1)
            dve.wait_ge(of_pe, 2)
            dve.wait_ge(w_in, 64)
            link(dve.scalar_tensor_tensor(prod[:], w1[:], 1.0, cps[0:HID, 0:F], ALU.mult, ALU.mult,
                                          accum_out=h[:, 0:1]))
            dve.tensor_scalar(h[:, 1:2], h[:, 0:1], b1[:], 0.0, ALU.add, ALU.max).then_inc(to_pe, 1)
            dve.wait_ge(of_pe, 3)
            link(dve.tensor_tensor(lg[:, 0:NCOEF], cps[0:1, 0:NCOEF], b2[:], ALU.add))
            link(dve.tensor_reduce(tiny[:, 4:5], lg[:, 0:NCOEF], AX.X, ALU.max))
            dve.tensor_scalar(lg[:, 0:NCOEF], lg[:, 0:NCOEF], tiny[:, 4:5], None, ALU.subtract).then_inc(to_act, 1)
            dve.wait_ge(of_act, 2)
            link(dve.tensor_reduce(tiny[:, 5:6], cf[:, 0:NCOEF], AX.X, ALU.add))
            link(dve.reciprocal(tiny[:, 6:7], tiny[:, 5:6]))
            link(dve.tensor_scalar(cf[:, 0:NCOEF], cf[:, 0:NCOEF], tiny[:, 6:7], None, ALU.mult))
            link(dve.memset(cf[:, 7:8], 0.0))
            dve.tensor_scalar(cf[:, 6:7], cf[:, 0:1], 1.0, None, ALU.add).then_inc(to_pe, 1)
            dve.wait_ge(of_pe, 4)
            link(dve.tensor_copy(k.coef[:], cps[:, 0:8]))

        @block.scalar
        def _(act):
            act.wait_ge(to_act, 1)
            act.activation(feat[:, C + 1:C + 2], tiny[:, 3:4], ACT.Sqrt).then_inc(of_act, 1)
            act.wait_ge(to_act, 2)
            act.activation(cf[:, 0:NCOEF], lg[:, 0:NCOEF], ACT.Exp).then_inc(of_act, 1)

        @block.tensor
        def _(pe):
            pe.wait_ge(to_pe, 1)
            pe.matmul(cps[0:1, 0:1], qs[:], k.ones[0:NP, 0:1], start=True, stop=True).then_inc(of_pe, 1)
            pe.wait_ge(to_pe, 2)
            pe.matmul(cps[0:HID, 0:F], k.ones[0:1, 0:HID], feat[:], start=True, stop=True).then_inc(of_pe, 1)
            pe.wait_ge(to_pe, 3)
            pe.wait_ge(w_in, 64)
            pe.matmul(cps[0:1, 0:NCOEF], h[:, 1:2], w2[:], start=True, stop=True).then_inc(of_pe, 1)
            pe.wait_ge(to_pe, 4)
            pe.matmul(cps[:, 0:8], k.ones[0:1, 0:P], cf[:], start=True, stop=True).then_inc(of_pe, 1)


_INS = ['x', 'src', 'dst', 'L0_gnn_W', 'L0_gnn_b', 'L1_gnn_W1', 'L1_gnn_b1', 'L1_gnn_W2', 'L1_gnn_b2']


def kernel(**inputs):
    import numpy as _np
    import concourse.bacc as _bacc
    from concourse import mybir as _mybir
    from concourse.bass_utils import run_bass_kernel_spmd as _run

    nc = _bacc.Bacc("TRN2", target_bir_lowering=False, num_devices=1)
    arrays, args = {}, []
    for name in _INS:
        a = _np.ascontiguousarray(inputs[name])
        arrays[f"in_{name}"] = a
        args.append(nc.dram_tensor(f"in_{name}", a.shape, _mybir.dt.from_np(a.dtype), kind="ExternalInput").ap())
    args.append(nc.dram_tensor("out_x", (N, C), _mybir.dt.float32, kind="ExternalOutput").ap())
    build(nc, *args)
    r = _run(nc, [arrays], core_ids=[0])
    return r.results[0]["out_x"]
```

```python
from contextlib import ExitStack, contextmanager

import concourse.bass as bass
from concourse import mybir

FP32, FP16, BF16 = mybir.dt.float32, mybir.dt.float16, mybir.dt.bfloat16
I32, U32, U8 = mybir.dt.int32, mybir.dt.uint32, mybir.dt.uint8
ALU = mybir.AluOpType
ACT = mybir.ActivationFunctionType
AX = mybir.AxisListType
ds = bass.ds

P = 128
N = 100000
C = 64
E = 50000
HID = 32
NCOEF = 6
EPS = 1e-5
NEG = -1e30
ROUND = 12582912.0
FAR = float(1 << 20)

NP = 125
NC = N // NP
NR = NC // 2
NROW = 2 * NP
BANK = 512

ET = 392
EB = ET // 4
EARLY = 3
GT = 4
GPOS = GT * P
NG = 100
NT = NG * GT
NPOS = NG * GPOS
assert E + 2 * GPOS <= NPOS
BLK = 4
ZERO_ROW = NPOS
REC = 408 * P
REC_W = 17
FILLS = 50
FILL_W = N * C // P // FILLS
EXT = C + 2
KN = 10
NCH = NC // KN
NBUF = 4
SPLIT = (0, 112, NP)


def bc(ap, n):
    return ap.unsqueeze(2).to_broadcast([ap.shape[0], ap.shape[1], n])


@contextmanager
def semaphores(nc):
    held = []

    def sem(name):
        held.append(nc.alloc_semaphore(name))
        return held[-1]

    yield sem
    nc.clear_and_free_semaphores(held)
    nc.all_engine_barrier()


class Names:
    pass


class Chain:

    def __init__(self, eng, sem):
        self.eng, self.sem, self.n = eng, sem, 0

    def __call__(self, instruction):
        instruction.then_inc(self.sem, 1)
        self.n += 1
        self.eng.wait_ge(self.sem, self.n)


def settle(eng, k, *values):
    for v in values:
        eng.lower_val(v)
    eng.wait_ge(k.begun, 1)
    return values


def node_dma(eng, sem, dst, src):
    for a, b in zip(SPLIT, SPLIT[1:]):
        eng.dma_start(dst(a, b), src(a, b)).then_inc(sem, 16)


def build(nc, x, src, dst, W0, b0, W1, b1, W2, b2, out):
    def dram(name, shape, dt):
        return nc.dram_tensor(name, shape, dt).ap()

    d = Names()
    d.x, d.src, d.dst, d.out = x, src, dst, out
    d.W0, d.b0, d.W1, d.b1, d.W2, d.b2 = W0, b0, W1, b1, W2, b2
    d.src_rows = dram("src_rows", [ET * P], FP32)
    d.hi_rows = dram("hi_rows", [ET * P], FP32)
    d.rec = dram("rec", [REC, EXT], FP32)
    d.marks = dram("marks", [BLK * P * P], U8)
    d.node_max = dram("node_max", [N, C], FP32)
    d.node_sum = dram("node_sum", [N, C], FP32)
    d.x1 = dram("x1", [N + 1, EXT], FP32)
    d.tab = [dram(f"tab{t}", [NPOS + P, C], FP32) for t in range(2)]
    with ExitStack() as keep:
        def sb(name, shape, dt=FP32):
            return keep.enter_context(nc.sbuf_tensor(name, shape, dt))

        k = Names()
        k.ident, k.upper, k.ones = sb("ident", [P, P]), sb("upper", [P, P]), sb("ones", [P, P])
        k.iota = sb("iota", [P, NR], FP16)
        k.D, k.last, k.qsum = sb("D", [NP, NC]), sb("last", [NP, NC]), sb("qsum", [NP, NC])
        ahead = 2 * GT
        k.dst_at = sb("dst_at", [P, BLK * P + ahead], U32)
        k.to = sb("to", [P, BLK * P], U32)
        k.last_at, k.w = sb("last_at", [P, NT + ahead], U32), sb("w", [P, NT])
        k.coef, k.eps, k.rounds = sb("coef", [P, 8]), sb("eps", [P, 1]), sb("rounds", [1, 1], I32)
        k.Wd, k.Wb = sb("Wd", [P, P]), sb("Wb", [C + 1, C])
        k.begun = nc.alloc_semaphore("begun")
        count_and_place(nc, d, k)
        with nc.sbuf_tensor("cont", [C, NPOS], U8) as cont:
            k.cont = cont
            read_records(nc, d, k)
            edge_pass(nc, d, k, "M", stream=d.rec, scatter=d.node_max)
            with ExitStack() as scope:
                node_pass(nc, d, k, scope, 0)
                mixing(nc, d, k, scope)
            with nc.sbuf_tensor("Xd", [P, NT, C], FP32) as Xd:
                k.Xd = Xd
                edge_pass(nc, d, k, "H5", gather=d.x1, store=d.tab[0], coef=5)
                for step in (4, 3, 2):
                    edge_pass(nc, d, k, f"H{step}", gather=d.tab[step % 2], store=d.tab[1 - step % 2],
                              coef=step, inner=True)
                edge_pass(nc, d, k, "H1", gather=d.tab[1], scatter=d.node_sum, coef=1)
        with ExitStack() as scope:
            node_pass(nc, d, k, scope, 1)


def count_and_place(nc, d, k):
    with ExitStack() as scope:
        def sb(name, shape, dt=FP32):
            return scope.enter_context(nc.sbuf_tensor(name, shape, dt))

        sem = scope.enter_context(semaphores(nc))
        recs = sb("recs", [P, BLK * P, 2])
        hi = sb("hi", [P, 2, BLK * P])
        lo = sb("lo", [P, 2, BLK * P])
        pen = sb("pen", [P, BLK * P])
        mask = sb("mask", [P, GPOS])
        part = sb("part", [P, 2])
        fill = sb("fill", [P, FILL_W])
        edge_x = sb("edge_x", [P, EB, EARLY, C])
        x_at = sb("x_at", [P, ET + 8], U32)
        rec0 = sb("rec0", [P, REC_W, EXT])
        zrow = sb("zrow", [P, C])
        xpad = sb("xpad", [1, EXT])
        start = sb("start", [NP, 2, NC])

        init = sem("init")
        fills, rec_filled = sem("fills"), sem("rec_filled")
        const_ready, ids_ready, ids_blank = sem("const_ready"), sem("ids_ready"), sem("ids_blank")
        rows_ready, rows_stored = sem("rows_ready"), sem("rows_stored")
        tr_done, tr_free, keys_ready = sem("tr_done"), sem("tr_free"), sem("keys_ready")
        vch, pch = sem("vch"), sem("pch")

        with (nc.sbuf_tensor("ids", [P, 2, BLK, P], I32) as ids,
              nc.sbuf_tensor("id_rows", [P, 2, BLK, P], FP32) as rows,
              nc.sbuf_tensor("hirow", [P, BLK, P], FP32) as hirow,
              nc.psum_tensor("tr_ps", [P, 4, BANK], FP32) as tr_ps, nc.Block() as block):
            @block.gpsimd
            def _(pool):
                pool.sem_inc(k.begun, 1)
                link = Chain(pool, pch)
                pool.memset(fill[:], NEG).then_inc(init, 1)
                pool.memset(zrow[:], 0.0).then_inc(init, 1)
                link(pool.memset(xpad[:], 0.0))
                pool.memset(xpad[:, C + 1:C + 2], float(ZERO_ROW)).then_inc(init, 1)
                link(pool.memset(k.ident[:], 0.0))
                link(pool.affine_select(out=k.ident[:], in_=k.ident[:], compare_op=ALU.not_equal, fill=1.0,
                                        base=0, pattern=[[-1, P]], channel_multiplier=1))
                link(pool.memset(k.upper[:], 1.0))
                link(pool.affine_select(out=k.upper[:], in_=k.upper[:], compare_op=ALU.is_gt, fill=0.0,
                                        base=0, pattern=[[1, P]], channel_multiplier=-1))
                link(pool.memset(mask[:], 1.0))
                link(pool.affine_select(out=mask[:], in_=mask[:], compare_op=ALU.is_gt, fill=0.0,
                                        base=GPOS - P, pattern=[[-1, GPOS]], channel_multiplier=1))
                pool.iota(part[:], [[-1, 2]], base=0, channel_multiplier=-2, allow_small_or_imprecise_dtypes=True)
                pool.iota(k.iota[:], [[1, NR]], base=0, channel_multiplier=0, allow_small_or_imprecise_dtypes=True)
                pool.memset(k.eps[:], EPS)
                pool.memset(k.ones[:], 1.0).then_inc(const_ready, 1)

            @block.vector
            def _(dve):
                link = Chain(dve, vch)
                dve.memset(ids[:], -1).then_inc(ids_blank, 1)
                link(dve.memset(rec0[:], 0.0))
                dve.memset(rec0[:, :, C:EXT], float(N)).then_inc(init, 1)
                dve.memset(x_at[:, ET:], 0)
                dve.wait_ge(ids_ready, 16 * 10)
                link(dve.tensor_copy(rows[:], ids[:]))
                link(dve.tensor_scalar(hirow[:], rows[:, 0], -(NR - 1) / 2, 1.0 / NR, ALU.add, ALU.mult))
                dve.tensor_scalar(hirow[:], hirow[:], ROUND, ROUND, ALU.add, ALU.subtract).then_inc(rows_ready, 1)
                for which in range(2):
                    dve.wait_ge(tr_done, which + 1)
                    link(dve.tensor_copy(recs[:, :, 1 - which], tr_ps[:, which, :]))
                    v, h, l = recs[:, :, 1 - which], hi[:, which], lo[:, which]
                    link(dve.tensor_scalar(h, v, -(NR - 1) / 2, 1.0 / NR, ALU.add, ALU.mult))
                    link(dve.tensor_scalar(h, h, ROUND, ROUND, ALU.add, ALU.subtract))
                    link(dve.scalar_tensor_tensor(l, h, float(-NR), v, ALU.mult, ALU.add))
                dve.tensor_scalar(x_at[:, 0:ET], recs[:, 0:ET, 0], 0.0, None, ALU.max)
                link(dve.tensor_scalar(pen[:], recs[:, :, 1], 0.0, FAR, ALU.is_lt, ALU.mult))
                dve.tensor_scalar(pen[:], pen[:], 1.0, None, ALU.add).then_inc(keys_ready, 1)

            @block.tensor
            def _(pe):
                pe.wait_ge(const_ready, 1)
                pe.wait_ge(rows_ready, 1)
                for which in range(2):
                    for b in range(BLK):
                        last = pe.transpose(tr_ps[:, which, b * P:(b + 1) * P], rows[:, which, b, :], k.ident[:])
                    last.then_inc(tr_done, 1)

            @block.sync
            def _(sp):
                sp.wait_ge(ids_blank, 1)
                full = E // P
                for which, v in enumerate((d.src, d.dst)):
                    for b in range(BLK - 1):
                        sp.dma_start(ids[:, which, b, :], v[b * P * P:(b + 1) * P * P].rearrange("(t e) -> t e", e=P)
                                     ).then_inc(ids_ready, 16)
                    t = (BLK - 1) * P
                    sp.dma_start(ids[0:full - t, which, BLK - 1, :], v[t * P:full * P].rearrange("(t e) -> t e", e=P)
                                 ).then_inc(ids_ready, 16)
                    sp.dma_start(ids[full - t:full - t + 1, which, BLK - 1, 0:E - full * P],
                                 v[full * P:E].unsqueeze(0)).then_inc(ids_ready, 16)
                sp.wait_ge(rows_ready, 1)
                for tab, rws in ((d.src_rows, rows[:, 0]), (d.hi_rows, hirow[:, :, :])):
                    for b in range(BLK):
                        n = min(P, ET - b * P)
                        sp.dma_start(tab[b * P * P:(b * P + n) * P].rearrange("(t e) -> t e", e=P), rws[0:n, b, :]
                                     ).then_inc(rows_stored, 16)
                sp.wait_ge(rows_stored, 2 * BLK * 16)

        n_fills = 16 * (3 + FILLS)

        oh_ready, oh_used, far_done, dst_ready = (
            [sem(f"{nm}{s}") for s in range(2)] for nm in ("oh_ready", "oh_used", "far_done", "dst_ready"))
        zero_ready, counted, cch = sem("zero_ready"), sem("counted"), sem("cch")
        pref_in, pref_out = sem("pref_in"), sem("pref_out")
        at_ready, gathered, kept = ([sem(f"{nm}{s}") for s in range(2)] for nm in ("at_ready_x", "gathered_x", "kept_x"))
        with ExitStack() as inner:
            isb = lambda name, shape, dt=FP32: inner.enter_context(nc.sbuf_tensor(name, shape, dt))
            ohp = isb("ohp", [P, 2, 4, NROW], BF16)
            ohd = isb("ohd", [P, 2, 4, NROW], BF16)
            ohc = isb("ohc", [P, 2, 4, 2, NR], BF16)
            far = isb("far", [P, 2, 4, NROW])
            zero = isb("zero", [P, BANK], BF16)
            cnt = isb("cnt", [NP, 3, NC])
            at = isb("at_x", [P, 2, EARLY], U32)
            rows_x = isb("rows_x", [P, 2, EARLY, C])
            inn, cum, part1 = isb("inn", [NP, NC]), isb("cum", [NP, 2, NC]), isb("part1", [NP, 2, NC])
            onesc, both = isb("onesc", [NP, NC]), isb("both", [NP, NC])
            tot = isb("tot", [NP, 2])
            off = isb("off", [NP, 4])
            cps = [inner.enter_context(nc.psum_tensor(f"cps{w}", [NP, 2, BANK], FP32)) for w in range(3)]
            offps = inner.enter_context(nc.psum_tensor("offps", [NP, BANK], FP32))
            block = inner.enter_context(nc.Block())

            @block.vector
            def _(dve):
                dve.memset(zero[:], 0.0).then_inc(zero_ready, 1)
                with dve.Fori(0, EB // 2) as i:
                    for u in range(2):
                        dve.wait_ge(oh_used[u], i)
                        for j in range(4):
                            t = ds(i * 2 + u + j * EB, 1)
                            dve.tensor_scalar(ohp[:, u, j], k.iota[:, 0:NROW], hi[:, 0, t], None, ALU.is_equal)
                            for w in range(2):
                                last = dve.tensor_scalar(ohc[:, u, j, w], k.iota[:], lo[:, w, t], None, ALU.is_equal)
                            last.then_inc(oh_ready[u], 1)
                link = Chain(dve, cch)
                dve.wait_ge(counted, 1)
                for w in range(3):
                    link(dve.tensor_copy(cnt[:, w].rearrange("p (h c) -> p h c", h=2), cps[w][:, :, 0:NR]))
                link(dve.memset(onesc[:], 1.0))
                hs, hd = both[:], cnt[:, 2]
                link(dve.tensor_tensor(hs, cnt[:, 0], cnt[:, 1], ALU.add))
                link(dve.tensor_scalar(inn[:], hd, 0.0, None, ALU.is_gt))
                link(dve.tensor_tensor(part1[:, 0], hs, inn[:], ALU.mult))
                link(dve.tensor_tensor(part1[:, 1], hs, part1[:, 0], ALU.subtract))
                for w in range(2):
                    link(dve.tensor_tensor_scan(cum[:, w], onesc[:], part1[:, w], 0.0, ALU.mult, ALU.add))
                link(dve.tensor_copy(tot[:], cum[:, :, NC - 1]))
                dve.sem_inc(pref_in, 1)
                dve.wait_ge(pref_out, 1)
                link(dve.tensor_copy(off[:], offps[:, 0:4]))
                link(dve.tensor_scalar(off[:, 2:3], off[:, 2:3], 1.0 / (2 * GPOS), 0.5 - 0.5 / (2 * GPOS),
                                       ALU.mult, ALU.add))
                link(dve.tensor_scalar(off[:, 2:3], off[:, 2:3], ROUND, ROUND, ALU.add, ALU.subtract))
                link(dve.tensor_scalar(off[:, 2:3], off[:, 2:3], 1.0, None, ALU.max))
                link(dve.tensor_copy(k.rounds[:], off[0:1, 2:3]))
                link(dve.scalar_tensor_tensor(off[:, 1:2], off[:, 2:3], float(2 * GPOS), off[:, 1:2], ALU.mult, ALU.add))
                for w in range(2):
                    link(dve.scalar_tensor_tensor(cum[:, w], cum[:, w], off[:, w:w + 1], part1[:, w],
                                                  ALU.add, ALU.subtract))
                link(dve.tensor_tensor(cum[:, 0], cum[:, 0], cum[:, 1], ALU.subtract))
                link(dve.tensor_tensor(cum[:, 0], cum[:, 0], inn[:], ALU.mult))
                link(dve.tensor_tensor(start[:, 0], cum[:, 0], cum[:, 1], ALU.add))
                link(dve.tensor_tensor(start[:, 1], start[:, 0], cnt[:, 0], ALU.add))
                link(dve.tensor_scalar(inn[:], hs, 0.0, None, ALU.is_gt))
                link(dve.scalar_tensor_tensor(k.last[:], start[:, 0], float(-1 - ZERO_ROW), hs, ALU.add, ALU.add))
                link(dve.tensor_tensor(k.last[:], k.last[:], inn[:], ALU.mult))
                link(dve.tensor_scalar(k.last[:], k.last[:], float(ZERO_ROW), None, ALU.add))
                dve.tensor_scalar(k.D[:], hd, 1e-12, None, ALU.max).then_inc(pref_in, 1)
                dve.wait_ge(pref_out, 2)
                link(dve.reciprocal(k.D[:], k.D[:]))

            @block.gpsimd
            def _(pool):
                with pool.Fori(0, EB // 2) as i:
                    for s in range(2):
                        again, before = settle(pool, k, i + 1, i)
                        pool.wait_ge(at_ready[s], again)
                        pool.wait_ge(kept[s], before)
                        for j in range(EARLY):
                            pool.indirect_dma_start(
                                out=rows_x[:, s, j, :], out_offset=None, in_=d.x,
                                in_offset=bass.IndirectOffsetOnAxis(ap=at[:, s, j:j + 1], axis=0),
                            ).then_inc(gathered[s], 16)

            @block.scalar
            def _(act):
                def fetch(i, s):
                    act.wait_ge(gathered[s], i * (16 * EARLY))
                    act.activation(at[:, s], x_at[:, ds(i * 8 + s * 4, EARLY)], ACT.Copy).then_inc(at_ready[s], 1)

                def dst_rows(i, u):
                    act.wait_ge(dst_ready[u], i)
                    for j in range(4):
                        last = act.activation(far[:, u, j], k.iota[:, 0:NROW], ACT.Abs, scale=-1.0,
                                              bias=hi[:, 1, ds(i * 2 + u + j * EB, 1)])
                    last.then_inc(far_done[u], 1)
                    act.wait_ge(far_done[u], i + 1)
                    act.wait_ge(oh_used[u], i)
                    act.activation(ohd[:, u], far[:, u], ACT.Relu, bias=1.0, scale=-1.0).then_inc(dst_ready[u], 1)

                for s in range(2):
                    fetch(0, s)
                act.wait_ge(init, 4)
                act.dma_start(d.rec.rearrange("(p a r) f -> p a (r f)", p=P, r=REC_W),
                              rec0[:].rearrange("p r f -> p (r f)").unsqueeze(1).to_broadcast(
                                  [P, REC // P // REC_W, REC_W * EXT])).then_inc(rec_filled, 16)
                act.dma_start(d.x1[N:N + 1, :], xpad[:]).then_inc(fills, 16)
                for tab in d.tab:
                    act.dma_start(tab[NPOS:NPOS + P, :], zrow[:]).then_inc(fills, 16)
                with act.Fori(0, EB // 2) as i:
                    for s in range(2):
                        dst_rows(i, s)
                        fetch(i + 1, s)
                        act.activation(edge_x[:, ds(i * 2 + s, 1)].rearrange("p a j c -> p (a j) c"), rows_x[:, s],
                                       ACT.Copy).then_inc(kept[s], 1)
                act.wait_ge(pref_in, 2)
                act.activation(k.D[:], k.D[:], ACT.Sqrt).then_inc(pref_out, 1)

            @block.tensor
            def _(pe):
                pe.wait_ge(zero_ready, 1)
                for w in range(3):
                    for h in range(2):
                        pe.matmul(cps[w][:, h, 0:NR], zero[:, 0:NP], zero[:, 0:NR], start=True, stop=True)
                with pe.Fori(0, EB // 2) as i:
                    for u in range(2):
                        pe.wait_ge(dst_ready[u], i + 1)
                        for j in range(4):
                            pe.wait_ge(oh_ready[u], i * 4 + (j + 1))
                            for w, rows in enumerate((ohp, ohd)):
                                for h in range(2):
                                    last = pe.matmul(cps[2 if w else j // 2][:, h, 0:NR], rows[:, u, j, h::2],
                                                     ohc[:, u, j, w], start=False, stop=True, skip_group_check=True)
                        last.then_inc(oh_used[u], 1)
                for u in range(2):
                    pe.wait_ge(oh_used[u], EB // 2)
                pe.sem_inc(counted, 1)
                pe.wait_ge(pref_in, 1)
                pe.matmul(offps[:, 0:2], k.upper[0:NP, 0:NP], tot[:], start=True, stop=True)
                pe.matmul(offps[:, 2:4], k.ones[0:NP, 0:NP], tot[:], start=True, stop=True).then_inc(pref_out, 1)

        two = lambda name: [sem(f"{name}{s}") for s in range(2)]
        rows_in, rows_used, dist_done, hiT_ready = two("rows_in"), two("rows_used"), two("dist_done"), two("hiT_ready")
        onehots, added, table_ready = two("onehots"), two("added"), two("table_ready")
        pos_ready = two("pos_ready")
        got, got_read = [sem(f"got{j}") for j in range(4)], [sem(f"got_read{j}") for j in range(4)]
        rec_ready, scattered, based = two("rec_ready"), two("scattered"), two("based")
        seeded, high_ready, low_left = sem("seeded"), two("high_ready"), two("low_left")
        late_at_ready, late_done = two("late_at_ready"), two("late_done")
        with ExitStack() as inner:
            isb = lambda name, shape, dt=FP32: inner.enter_context(nc.sbuf_tensor(name, shape, dt))
            hibc, srcbc = isb("hibc", [P, 2, GPOS]), isb("srcbc", [P, 2, GPOS])
            dist = isb("dist", [NP, 2, GPOS])
            hiT = isb("hiT", [NP, 2, 2, GPOS], BF16)
            ohp = isb("ohp2", [P, 2, 4, NROW], BF16)
            ohc = isb("ohc2", [P, 2, 4, NR], BF16)
            table = isb("table", [NP, 2, 2, 2, NR], BF16)
            eye = isb("eye", [NP, 2, NP], BF16)
            late_at, late_x = isb("late_at", [P, 2, 1], U32), isb("late_x", [P, 2, C])
            eq = isb("eq", [P, 4, GPOS], BF16)
            picked = isb("picked", [P, 4, NR], BF16)
            at, rank, base = isb("at", [P, 2, 4]), isb("rank", [P, 2, 4]), isb("base", [P, 2, 4])
            pos = isb("pos", [P, 2, 4], U32)
            rec = isb("rec_sb", [P, 2, 4, EXT])
            tps = [inner.enter_context(nc.psum_tensor(f"tps{s}", [NP, 2, BANK], FP32)) for s in range(2)]
            gps = [inner.enter_context(nc.psum_tensor(f"gps{j}", [P, BANK], FP32)) for j in range(4)]
            block = inner.enter_context(nc.Block())
            LAST = EB // 2 - 1

            @block.sync
            def _(sp):
                parts = d.node_max.rearrange("r f -> (r f)").rearrange("(p w) -> p w", p=P)
                sp.wait_ge(init, 4)
                for c in range(EB // 2, FILLS):
                    sp.dma_start(parts[:, c * FILL_W:(c + 1) * FILL_W], fill[:]).then_inc(fills, 16)
                with sp.Fori(0, EB // 2) as i:
                    sp.dma_start(parts[:, ds(i * FILL_W, FILL_W)], fill[:]).then_inc(fills, 16)
                    for s in range(2):
                        before, twice = settle(sp, k, i, i * 2)
                        sp.wait_ge(rows_used[s], before)
                        sp.wait_ge(dist_done[s], twice)
                        for to, of in ((hibc, d.hi_rows), (srcbc, d.src_rows)):
                            sp.dma_start(to[:, s], of[ds(i * GPOS + s * (ET // 2 * P), GPOS)].partition_broadcast(P)
                                         ).then_inc(rows_in[s], 16)
                sp.wait_ge(fills, n_fills)

            @block.vector
            def _(dve):
                def prepare(i, s):
                    dve.wait_ge(rows_in[s], i * 32 + 32)
                    for j in range(4):
                        t, n = ds(i * 4 + s * (ET // 2) + j, 1), (j + 1) * P
                        last = dve.scalar_tensor_tensor(eq[:, j, 0:n], srcbc[:, s, 0:n], recs[:, t, 1],
                                                        mask[:, GPOS - n:GPOS], ALU.is_equal, ALU.mult,
                                                        accum_out=rank[:, s, j:j + 1])
                    last.then_inc(rows_used[s], 1)
                    dve.wait_ge(added[s], i)
                    for j in range(4):
                        t = ds(i * 4 + s * (ET // 2) + j, 1)
                        dve.tensor_scalar(ohp[:, s, j], k.iota[:, 0:NROW], hi[:, 0, t], None, ALU.is_equal)
                        last = dve.tensor_scalar(ohc[:, s, j], k.iota[:], lo[:, 0, t], None, ALU.is_equal)
                    last.then_inc(onehots[s], 1)
                    dve.wait_ge(rows_used[s], i + 1)
                    dve.wait_ge(pos_ready[s], i)
                    dve.tensor_tensor(base[:, s], rank[:, s], pen[:, ds(i * 4 + s * (ET // 2), 4)], ALU.add
                                      ).then_inc(based[s], 1)

                def place(i, s):
                    dve.wait_ge(onehots[s], i + 1)
                    for j in range(4):
                        dve.wait_ge(got[j], i * 2 + s + 1)
                        dve.scalar_tensor_tensor(picked[:, j], gps[j][:, 0:NR], 1.0, ohc[:, s, j],
                                                 ALU.mult, ALU.mult, accum_out=at[:, s, j:j + 1]
                                                 ).then_inc(got_read[j], 1)
                    for j in range(4):
                        dve.wait_ge(got_read[j], i * 2 + s + 1)
                    dve.wait_ge(based[s], i + 1)
                    dve.wait_ge(scattered[s], i * 64)
                    dve.tensor_tensor(pos[:, s], at[:, s], base[:, s], ALU.add).then_inc(pos_ready[s], 1)

                prepare(0, 0)
                with dve.Fori(0, LAST) as i:
                    prepare(i, 1)
                    place(i, 0)
                    prepare(i + 1, 0)
                    place(i, 1)
                prepare(LAST, 1)
                place(LAST, 0)
                place(LAST, 1)

            @block.tensor
            def _(pe):
                def high_part(s, sign):
                    for h in range(2):
                        last = pe.matmul(tps[s][:, h, 0:NR], eye[:, sign], table[:, s, 0, h],
                                         start=False, stop=True, skip_group_check=True)
                    return last

                for s in range(2):
                    for h in range(2):
                        last = pe.matmul(tps[s][:, h, 0:NR], k.ident[0:NP, 0:NP], start[:, s, h * NR:(h + 1) * NR],
                                         start=True, stop=True)
                last.then_inc(seeded, 1)
                pe.wait_ge(high_ready[0], 1)
                high_part(0, 1).then_inc(low_left[0], 1)
                with pe.Fori(0, EB // 2) as i:
                    for s in range(2):
                        pe.wait_ge(hiT_ready[s], i + 1)
                        pe.wait_ge(table_ready[s], i + 1)
                        for j in range(4):
                            pe.wait_ge(got_read[j], i * 2 + s)
                            for h in range(2):
                                for w in range(2):
                                    last = pe.matmul(gps[j][:, 0:NR], hiT[:, s, h, j * P:(j + 1) * P], table[:, s, w, h],
                                                     start=h + w == 0, stop=h + w == 2)
                            last.then_inc(got[j], 1)
                        high_part(s, 0)
                        pe.wait_ge(high_ready[1 - s], i + s + 1)
                        high_part(1 - s, 1).then_inc(low_left[1 - s], 1)
                        pe.wait_ge(onehots[s], i + 1)
                        for j in range(4):
                            for h in range(2):
                                last = pe.matmul(tps[s][:, h, 0:NR], ohp[:, s, j, h::2], ohc[:, s, j],
                                                 start=False, stop=True, skip_group_check=True)
                        last.then_inc(added[s], 1)

            @block.scalar
            def _(act):
                def rows(i, s):
                    act.wait_ge(rows_in[s], i * 32 + 32)
                    act.wait_ge(hiT_ready[1 - s], i + s)
                    for h in range(2):
                        act.activation(dist[:, h], hibc[0:NP, s], ACT.Abs, bias=part[0:NP, h:h + 1]
                                       ).then_inc(dist_done[s], 1)
                    act.wait_ge(dist_done[s], i * 2 + 2)
                    act.wait_ge(added[s], i)
                    act.activation(hiT[:, s], dist[:], ACT.Relu, bias=1.0, scale=-1.0).then_inc(hiT_ready[s], 1)

                def fetch(i, s):
                    act.wait_ge(late_done[s], i * 16)
                    act.activation(late_at[:, s], x_at[:, ds(i * 4 + s * (ET // 2) + EARLY, 1)], ACT.Copy
                                   ).then_inc(late_at_ready[s], 1)

                def records(i, s):
                    fetch(i + 1, s)
                    act.wait_ge(scattered[s], i * 64)
                    act.activation(rec[:, s, 0:EARLY, 0:C], edge_x[:, ds(i + s * (EB // 2), 1)]
                                   .rearrange("p a j c -> p (a j) c"), ACT.Copy)
                    act.activation(rec[:, s, EARLY, 0:C], late_x[:, s], ACT.Copy)
                    act.activation(rec[:, s, :, C:EXT], recs[:, ds(i * 4 + s * (ET // 2), 4), :], ACT.Copy
                                   ).then_inc(rec_ready[s], 1)

                def high(s, batches):
                    act.wait_ge(added[s], batches)
                    act.activation(table[:, s, 0], tps[s][:, :, 0:NR], ACT.Copy).then_inc(high_ready[s], 1)

                def low(s, batches):
                    act.wait_ge(low_left[s], batches + 1)
                    act.activation(table[:, s, 1], tps[s][:, :, 0:NR], ACT.Copy).then_inc(table_ready[s], 1)

                for sign in range(2):
                    act.activation(eye[:, sign], k.ident[0:NP, 0:NP], ACT.Copy, scale=1.0 - 2.0 * sign)
                for s in range(2):
                    fetch(0, s)
                rows(0, 0)
                act.wait_ge(seeded, 1)
                high(0, 0)
                low(0, 0)
                with act.Fori(0, LAST) as i:
                    for s in range(2):
                        high(1 - s, i + s)
                        records(i, s)
                        rows(i + s, 1 - s)
                        low(1 - s, i + s)
                high(1, LAST)
                records(LAST, 0)
                rows(LAST, 1)
                low(1, LAST)
                high(0, LAST + 1)
                records(LAST, 1)

            @block.gpsimd
            def _(pool):
                pool.wait_ge(rec_filled, 16)
                def gather(s):
                    pool.indirect_dma_start(
                        out=late_x[:, s, :], out_offset=None, in_=d.x,
                        in_offset=bass.IndirectOffsetOnAxis(ap=late_at[:, s], axis=0),
                    ).then_inc(late_done[s], 16)

                for s in range(2):
                    pool.wait_ge(late_at_ready[s], 1)
                    gather(s)
                with pool.Fori(0, EB // 2) as i:
                    for s in range(2):
                        again, twice = settle(pool, k, i + 1, i + 2)
                        pool.wait_ge(pos_ready[s], again)
                        pool.wait_ge(rec_ready[s], again)
                        for j in range(4):
                            pool.indirect_dma_start(
                                out=d.rec, out_offset=bass.IndirectOffsetOnAxis(ap=pos[:, s, j:j + 1], axis=0),
                                in_=rec[:, s, j, :], in_offset=None, bounds_check=REC - 1, oob_is_err=False,
                            ).then_inc(scattered[s], 16)
                        settle(pool, k)
                        pool.wait_ge(late_at_ready[s], twice)
                        gather(s)
                for s in range(2):
                    pool.wait_ge(scattered[s], EB // 2 * 64)
                    pool.wait_ge(late_done[s], (EB // 2 + 1) * 16)


def read_records(nc, d, k):
    with ExitStack() as scope:
        def sb(name, shape, dt=FP32):
            return scope.enter_context(nc.sbuf_tensor(name, shape, dt))

        sem = scope.enter_context(semaphores(nc))
        raw = sb("raw", [P, 2, P, EXT])
        ids = sb("ids3", [P, BLK, P + 2, 2])
        same = sb("same", [P, BLK, P], U8)
        val = sb("val", [P, 2, BLK, P])
        tmp = sb("tmp", [P, BLK, P])
        ps = [scope.enter_context(nc.psum_tensor(f"idx_ps{w}", [P, BANK], FP32)) for w in range(2)]
        loaded, taken, edges_in = [sem(f"loaded{s}") for s in range(2)], sem("taken"), sem("edges_in")
        blank, marked, stored, bcast = sem("blank"), sem("marked"), sem("stored"), sem("bcast")
        vch, tr_in, tr_out = sem("vch3"), sem("tr_in3"), sem("tr_out3")
        wa, wb = sb("wa", [P, C]), sb("wb", [P, C])
        weights_in, pch = sem("weights_in"), sem("pch3")
        block = scope.enter_context(nc.Block())

        @block.sync
        def _(sp):
            sp.wait_ge(blank, 1)
            tiles = d.rec[1:1 + NPOS, :].rearrange("(t p) f -> t p f", p=P)
            with nc.allow_non_contiguous_dma(reason="two ids for each tile"):
                for b in range(BLK):
                    n = min(P, NT - b * P)
                    for end, at in ((0, b * P * P), (P + 1, b * P * P + P + 1)):
                        v = d.rec[at:at + n * P, C:EXT].rearrange("(t p) f -> t p f", p=P)
                        sp.dma_start(ids[0:n, b, end, :], v[:, 0, :]).then_inc(edges_in, 16)
            for b in range(BLK):
                n = min(P, NT - b * P)
                if b >= 2:
                    sp.wait_ge(taken, b - 1)
                sp.dma_start(raw[0:n, b % 2], tiles[b * P:b * P + n]).then_inc(loaded[b % 2], 16)
            sp.wait_ge(marked, 1)
            sp.dma_start(d.marks.rearrange("(b t p) -> t b p", t=P, p=P), same[:]).then_inc(stored, 16)
            sp.wait_ge(stored, 16)
            q = NPOS // 4
            for c in range(4):
                sp.dma_start(k.cont[:, c * q:(c + 1) * q], d.marks[c * q:(c + 1) * q].partition_broadcast(C)
                             ).then_inc(bcast, 16)
            sp.wait_ge(bcast, 64)

        @block.vector
        def _(dve):
            link = Chain(dve, vch)
            dve.memset(ids[:], 0.0).then_inc(blank, 1)
            dve.memset(k.dst_at[:, BLK * P:], 0)
            dve.memset(k.last_at[:, NT:], 0)
            dve.wait_ge(blank, 1)
            for b in range(BLK):
                n = min(P, NT - b * P)
                dve.wait_ge(loaded[b % 2], 16 * (b // 2 + 1))
                dve.tensor_copy(ids[0:n, b, 1:P + 1, :], raw[0:n, b % 2, :, C:EXT]).then_inc(taken, 1)
            dve.wait_ge(taken, BLK)
            dve.wait_ge(edges_in, 2 * BLK * 16)
            src_of = lambda shift: ids[:, :, shift:shift + P, 1]
            dve.tensor_tensor(same[:], src_of(1), src_of(0), ALU.is_equal).then_inc(marked, 1)
            link(dve.tensor_copy(val[:, 0], ids[:, :, 1:P + 1, 0]))
            link(dve.tensor_tensor(tmp[:], src_of(1), src_of(2), ALU.is_equal))
            dve.scalar_tensor_tensor(val[:, 1], tmp[:], FAR, src_of(1), ALU.mult, ALU.add).then_inc(tr_in, 1)
            dve.wait_ge(tr_out, 1)
            dve.tensor_copy(k.dst_at[:, 0:BLK * P], ps[0][:])
            link(dve.tensor_copy(k.to[:, 0:BLK * P], ps[1][:]))

        @block.tensor
        def _(pe):
            pe.wait_ge(tr_in, 1)
            for w in range(2):
                for b in range(BLK):
                    last = pe.transpose(ps[w][:, b * P:(b + 1) * P], val[:, w, b, :], k.ident[:])
            last.then_inc(tr_out, 1)

        @block.scalar
        def _(act):
            act.dma_start(k.Wb[0:C, :], d.W0[C:2 * C, :]).then_inc(weights_in, 16)
            act.dma_start(k.Wb[C:C + 1, :], d.b0.unsqueeze(0)).then_inc(weights_in, 16)
            for h in range(2):
                act.dma_start(wa[h * C:(h + 1) * C, :], d.W0[0:C, :]).then_inc(weights_in, 16)
                act.dma_start(wb[h * C:(h + 1) * C, :], d.W0[C:2 * C, :]).then_inc(weights_in, 16)
            act.wait_ge(weights_in, 6 * 16)

        @block.gpsimd
        def _(pool):
            link = Chain(pool, pch)
            link(pool.memset(k.Wd[:], 0.0))
            pool.wait_ge(weights_in, 6 * 16)
            for h in range(2):
                a, b = h * C, (h + 1) * C
                link(pool.tensor_tensor(k.Wd[a:b, a:b], wa[a:b, :], wb[a:b, :], ALU.subtract))


def edge_pass(nc, d, k, name, gather=None, stream=None, store=None, scatter=None, coef=None, inner=False):
    project, first = stream is not None, coef == 5
    width = EXT if first or project else C
    with ExitStack() as scope:
        def sb(nm, shape, dt=FP32):
            return scope.enter_context(nc.sbuf_tensor(f"{nm}_{name}", shape, dt))

        def ps(nm, shape):
            return [scope.enter_context(nc.psum_tensor(f"{nm}{s}_{name}", shape, FP32)) for s in range(2)]

        sem = scope.enter_context(semaphores(nc))

        def two(nm):
            return [sem(f"{nm}{s}_{name}") for s in range(2)]

        at = sb("at", [P, 2, GT], U32)
        to = sb("to", [P, 2, GT], U32) if scatter is not None else None
        rows = sb("rows", [P, 2, GT, width])
        own = sb("own", [P, 2, GT, C]) if not project and not first else None
        z = sb("z", [P, 2, GT, C]) if not project else rows
        sums = sb("sums", [C, 2, GPOS])
        back = sb("back", [P, 2, GT, C])
        zT = ps("zT", [C, BANK])
        backT = ps("backT", [P, BANK])
        if project:
            zeros = sb("zeros", [P, FILL_W])
            fills, zeros_set = sem("fills_M"), sem("zeros_set")
            xT = sb("xT", [C + 1, 2, GPOS])
            pen = sb("pen", [C, 2, GPOS])
            vT = ps("vT", [C, BANK])
            xT_ready, pen_ready, vT_done = two("xT_ready"), two("pen_ready"), two("vT_done")
        at_ready, gathered = two("at_ready"), two("gathered")
        own_ready, z_ready, zT_done = two("own_ready"), two("z_ready"), two("zT_done")
        scanned, backT_done, back_ready = two("scanned"), two("backT_done"), two("back_ready")
        away = two("away")
        begun, ich = (sem(f"{nm}_{name}") for nm in ("begun", "ich"))
        at_table = k.dst_at if first else k.last_at
        LAST = NG // 2 - 1

        block = scope.enter_context(nc.Block())

        def rounds(eng):
            return eng.value_load(k.rounds[0:1, 0:1], min_val=1, max_val=NG // 2) if inner else NG // 2

        @block.gpsimd
        def _(pool):
            def gather_group(i, s):
                again, = settle(pool, k, i + 1)
                pool.wait_ge(at_ready[s], again)
                pool.wait_ge(z_ready[s], i)
                for j in range(GT):
                    pool.indirect_dma_start(
                        out=rows[:, s, j, :], out_offset=None, in_=gather,
                        in_offset=bass.IndirectOffsetOnAxis(ap=at[:, s, j:j + 1], axis=0),
                    ).then_inc(gathered[s], 16)

            def scatter_group(i, s):
                again, = settle(pool, k, i + 1)
                pool.wait_ge(back_ready[s], again)
                for j in range(GT):
                    pool.indirect_dma_start(
                        out=scatter, out_offset=bass.IndirectOffsetOnAxis(ap=to[:, s, j:j + 1], axis=0),
                        in_=back[:, s, j, :], in_offset=None, bounds_check=N - 1, oob_is_err=False,
                    ).then_inc(away[s], 16)

            if project:
                with pool.Fori(0, NG // 2) as i:
                    for s in range(2):
                        scatter_group(i, s)
            elif scatter is None:
                with pool.Fori(0, rounds(pool)) as i:
                    for s in range(2):
                        gather_group(i, s)
            else:
                for s in range(2):
                    gather_group(0, s)
                with pool.Fori(1, NG // 2) as i:
                    for s in range(2):
                        gather_group(i, s)
                        scatter_group(i - 1, s)
                for s in range(2):
                    scatter_group(NG // 2 - 1, s)
            if scatter is not None:
                for s in range(2):
                    pool.wait_ge(away[s], NG // 2 * GT * 16)

        @block.sync
        def _(sp):
            if project:
                sp.wait_ge(zeros_set, 1)
                parts = d.node_sum.rearrange("r f -> (r f)").rearrange("(p w) -> p w", p=P)
                with sp.Fori(0, NG // 2) as i:
                    sp.dma_start(parts[:, ds(i * FILL_W, FILL_W)], zeros[:]).then_inc(fills, 16)
                    sp.dma_start(d.tab[1][ds(i * (2 * GPOS), 2 * GPOS), :].rearrange("(p r) f -> p (r f)", p=P),
                                 zeros[:, 0:2 * GPOS * C // P]).then_inc(fills, 16)
                    for s in range(2):
                        before, = settle(sp, k, i)
                        sp.wait_ge(zT_done[s], before)
                        sp.dma_start(rows[:, s], stream[ds(i * (2 * GPOS) + s * GPOS + 1, GPOS), :]
                                     .rearrange("(j p) f -> p j f", p=P)).then_inc(gathered[s], 16)
                sp.wait_ge(fills, NG // 2 * 32)
            if store is not None:
                n = rounds(sp)
                with sp.Fori(0, n) as i:
                    for s in range(2):
                        sp.wait_ge(back_ready[s], i + 1)
                        sp.dma_start(store[ds(i * (2 * GPOS) + s * GPOS, GPOS), :].rearrange("(j p) f -> p j f", p=P),
                                     back[:, s]).then_inc(away[s], 16)
                landed, = settle(sp, k, n * 16)
                for s in range(2):
                    sp.wait_ge(away[s], landed)

        @block.scalar
        def _(act):
            def fetch(i, s):
                act.wait_ge(gathered[s], i * (GT * 16))
                act.activation(at[:, s], at_table[:, ds(i * (2 * GT) + s * GT, GT)], ACT.Copy
                               ).then_inc(at_ready[s], 1)

            def prepare(i, s):
                if project:
                    act.wait_ge(scanned[s], i)
                    act.activation(pen[:, s], k.cont[:, ds(i * (2 * GPOS) + s * GPOS, GPOS)], ACT.Copy,
                                   bias=NEG, scale=-NEG).then_inc(pen_ready[s], 1)
                elif not first:
                    act.wait_ge(z_ready[s], i)
                    act.activation(own[:, s], k.Xd[:, ds(i * (2 * GT) + s * GT, GT), :], ACT.Copy,
                                   scale=k.coef[:, coef:coef + 1]).then_inc(own_ready[s], 1)

            def turned(i, s):
                act.wait_ge(zT_done[s], i + 1)
                act.wait_ge(vT_done[s], i)
                act.activation(xT[0:C, s], zT[s][:], ACT.Copy).then_inc(xT_ready[s], 1)

            def give_back(i, s):
                act.wait_ge(backT_done[s], i + 1)
                act.wait_ge(away[s], i * (16 if scatter is None else 16 * GT))
                if scatter is not None:
                    act.activation(to[:, s], k.to[:, ds(i * (2 * GT) + s * GT, GT)], ACT.Copy)
                act.activation(back[:, s].rearrange("p j c -> p (j c)"), backT[s][:, 0:GT * C], ACT.Copy
                               ).then_inc(back_ready[s], 1)

            if project:
                prepare(0, 0)
                turned(0, 0)
                with act.Fori(0, LAST) as i:
                    for s in range(2):
                        prepare(i + s, 1 - s)
                        turned(i + s, 1 - s)
                        give_back(i, s)
                prepare(LAST, 1)
                turned(LAST, 1)
                for s in range(2):
                    give_back(LAST, s)
                return
            n = rounds(act)
            for s in range(2):
                fetch(0, s)
            with act.Fori(0, n) as i:
                prepare(i, 0)
                fetch(i + 1, 0)
                prepare(i, 1)
                give_back(i, 0)
                fetch(i + 1, 1)
                give_back(i, 1)

        @block.vector
        def _(dve):
            n = rounds(dve)
            if project:
                dve.memset(zeros[:], 0.0).then_inc(zeros_set, 1)
                dve.memset(xT[C:C + 1, :, :], 1.0).then_inc(begun, 1)
            dve.memset(sums[:, 1, GPOS - 1:GPOS], 0.0).then_inc(ich, 1)
            dve.wait_ge(ich, 1)
            with dve.Fori(0, n) as i:
                for s in range(2):
                    if not project:
                        dve.wait_ge(gathered[s], i * (GT * 16) + GT * 16)
                        dve.wait_ge(zT_done[s], i)
                        tiles = ds(i * (2 * GT) + s * GT, GT)
                    if first:
                        last_D = rows[:, s, :, C]
                        dve.tensor_copy(k.last_at[:, tiles], rows[:, s, :, C + 1])
                        dve.tensor_tensor(k.w[:, tiles], last_D, last_D, ALU.mult)
                        for j in range(GT):
                            D = rows[:, s, j, C:C + 1]
                            dve.tensor_scalar(k.Xd[:, ds(i * (2 * GT) + s * GT + j, 1), :].rearrange("p a c -> p (a c)"),
                                              rows[:, s, j, 0:C], D, None, ALU.mult)
                            last = dve.tensor_scalar(z[:, s, j], rows[:, s, j, 0:C], D, k.coef[:, 5:6],
                                                     ALU.mult, ALU.mult)
                        last.then_inc(z_ready[s], 1)
                    elif not project:
                        dve.wait_ge(own_ready[s], i + 1)
                        for j in range(GT):
                            last = dve.scalar_tensor_tensor(z[:, s, j], rows[:, s, j],
                                                            k.w[:, ds(i * (2 * GT) + s * GT + j, 1)],
                                                            own[:, s, j], ALU.mult, ALU.add)
                        last.then_inc(z_ready[s], 1)
                    dve.wait_ge((vT_done if project else zT_done)[s], i + 1)
                    dve.wait_ge(backT_done[s], i)
                    dve.wait_ge(scanned[1 - s], i + s)
                    state = sums[:, 1 - s, GPOS - 1:GPOS]
                    if project:
                        dve.wait_ge(pen_ready[s], i + 1)
                        dve.tensor_tensor_scan(sums[:, s], pen[:, s], vT[s][:], state, ALU.add, ALU.max
                                               ).then_inc(scanned[s], 1)
                    else:
                        cont = k.cont[:, ds(i * (2 * GPOS) + s * GPOS, GPOS)]
                        dve.tensor_tensor_scan(sums[:, s], cont, zT[s][:], state, ALU.mult, ALU.add
                                               ).then_inc(scanned[s], 1)

        @block.tensor
        def _(pe):
            def turn(i, s):
                again, rows_in = settle(pe, k, i + 1, i * 16 + 16)
                if project:
                    pe.wait_ge(gathered[s], rows_in)
                    pe.wait_ge(xT_ready[s], i)
                else:
                    pe.wait_ge(z_ready[s], again)
                    pe.wait_ge(scanned[s], i)
                for j in range(GT):
                    last = pe.transpose(zT[s][:, j * P:(j + 1) * P], z[:, s, j, 0:C], k.ident[:])
                last.then_inc(zT_done[s], 1)

            def product(i, s):
                pe.wait_ge(xT_ready[s], i + 1)
                pe.wait_ge(scanned[s], i)
                pe.matmul(vT[s][:], k.Wb[:], xT[:, s], start=True, stop=True).then_inc(vT_done[s], 1)

            def turn_back(i, s):
                again, = settle(pe, k, i + 1)
                pe.wait_ge(scanned[s], again)
                pe.wait_ge(back_ready[s], i)
                for j in range(GT):
                    last = pe.transpose(backT[s][:, j * C:(j + 1) * C], sums[:, s, j * P:(j + 1) * P],
                                        k.ident[0:C, 0:C])
                last.then_inc(backT_done[s], 1)

            if project:
                pe.wait_ge(begun, 1)
                turn(0, 0)
                product(0, 0)
                with pe.Fori(0, LAST) as i:
                    for s in range(2):
                        turn(i + s, 1 - s)
                        turn_back(i, s)
                        product(i + s, 1 - s)
                turn(LAST, 1)
                turn_back(LAST, 0)
                product(LAST, 1)
                turn_back(LAST, 1)
                return
            with pe.Fori(0, rounds(pe)) as i:
                for s in range(2):
                    turn(i, s)
                    turn_back(i, s)


def node_pass(nc, d, k, scope, layer):
    def sb(nm, shape, dt=FP32):
        return scope.enter_context(nc.sbuf_tensor(f"{nm}_n{layer}", shape, dt))

    def ps(nm, shape):
        return scope.enter_context(nc.psum_tensor(f"{nm}_n{layer}", shape, FP32))

    wide = EXT if layer else C
    xin = sb("xin", [NP, NBUF, KN, wide])
    agg = sb("agg", [NP, NBUF, KN, C])
    pre, y, cent, sq = (sb(nm, [NP, NBUF, KN, C]) for nm in ("pre", "y", "cent", "sq"))
    res = sb("res", [NP, NBUF, KN, C if layer else EXT])
    total, mean, ssq, std, rstd, rsq = (
        sb(nm, [NP, NBUF, KN]) for nm in ("total", "mean", "ssq", "std", "rstd", "rsq"))
    table = (d.x1[0:N, :] if layer else d.x).rearrange("(p c) f -> p c f", c=NC)
    edges = (d.node_sum if layer else d.node_max).rearrange("(p c) f -> p c f", c=NC)
    target = (d.out if layer else d.x1[0:N, :]).rearrange("(p c) f -> p c f", c=NC)
    if not layer:
        xT = sb("xT", [P, 2, KN // 2, P])
        xTp = ps("xTp", [P, KN // 2, P])
        ap = [ps(f"ap{s}", [NP, KN, C]) for s in range(2)]
        k.sums_ps = ps("sums", [1, BANK])
        zero = sb("zero", [P, BANK], BF16)

    with ExitStack() as sems:
        sem = sems.enter_context(semaphores(nc))
        (loaded, pre_done, y_done, sum_done, mean_done, cent_done, sq_done, ssq_done, std_done, rstd_done, rsq_done,
         res_done, side, stored, xT_done, xT_ready, a_done, summed) = (
            [sem(f"{nm}{s}_n{layer}") for s in range(NBUF)] for nm in (
                "loaded", "pre_done", "y_done", "sum_done", "mean_done", "cent_done", "sq_done", "ssq_done", "std_done",
                "rstd_done", "rsq_done", "res_done", "side", "stored", "xT_done", "xT_ready", "a_done", "summed"))
        zeroed = sem(f"zeroed_n{layer}")
        sum2_done = [sem(f"sum2_done{s}_n{layer}") for s in range(NBUF)]
        block = sems.enter_context(nc.Block())

        def columns(i, s):
            return ds(i * (NBUF * KN) + s * KN, KN)

        def staggered(eng, *steps):
            most = max(lag for lag, _ in steps)
            assert most <= NBUF

            def turn(i, s):
                for lag, step in steps:
                    if isinstance(i, int) and not 0 <= NBUF * i + s - lag < NCH:
                        continue
                    step(i, s - lag) if s >= lag else step(i - 1, s - lag + NBUF)

            for s in range(NBUF):
                turn(0, s)
            with eng.Fori(1, NCH // NBUF) as i:
                for s in range(NBUF):
                    turn(i, s)
            for s in range(most):
                turn(NCH // NBUF, s)

        def before(i, s, n, sems):
            if s >= n:
                return sems[s - n], i + 1
            if isinstance(i, int) and i == 0:
                return None
            return sems[s - n + NBUF], i

        def wait_before(eng, i, s, n, sems):
            found = before(i, s, n, sems)
            if found:
                eng.wait_ge(*found)

        @block.sync
        def _(sp):
            def load(i, s):
                cols = columns(i, s)
                sp.wait_ge(y_done[s], i)
                if not layer:
                    sp.wait_ge(xT_done[s], i)
                node_dma(sp, loaded[s], lambda a, b: xin[a:b, s], lambda a, b: table[a:b, cols, :])
                node_dma(sp, loaded[s], lambda a, b: agg[a:b, s], lambda a, b: edges[a:b, cols, :])

            def store(i, s):
                cols = columns(i, s)
                sp.wait_ge(res_done[s], i + 1)
                if not layer:
                    sp.wait_ge(side[s], i + 1)
                node_dma(sp, stored[s], lambda a, b: target[a:b, cols, :], lambda a, b: res[a:b, s])

            staggered(sp, (0, load), (4, store))
            for s in range(NBUF):
                sp.wait_ge(stored[s], NCH // NBUF * 32)

        @block.gpsimd
        def _(pool):
            def centre(i, s):
                pool.wait_ge(mean_done[s], i + 1)
                pool.wait_ge(res_done[s], i)
                pool.wait_ge(sq_done[s], i)
                pool.tensor_tensor(cent[:, s], y[:, s], bc(mean[:, s], C), ALU.subtract).then_inc(cent_done[s], 1)

            def scale(i, s):
                pool.wait_ge(cent_done[s], i + 1)
                pool.wait_ge(rstd_done[s], i + 1)
                pool.wait_ge(stored[s], i * 32)
                if not layer:
                    pool.wait_ge(summed[s], i)
                pool.tensor_tensor(res[:, s, :, 0:C], cent[:, s], bc(rstd[:, s], C), ALU.mult).then_inc(res_done[s], 1)

            staggered(pool, (2, scale), (0, centre))

        @block.scalar
        def _(act):
            def turned(i, s):
                act.wait_ge(xT_done[s], i + 1)
                wait_before(act, i, s, 2, a_done)
                act.activation(xT[:, s % 2, :, 0:NP], xTp[:, :, 0:NP], ACT.Copy).then_inc(xT_ready[s], 1)

            def beside(i, s):
                act.wait_ge(stored[s], i * 32)
                act.activation(res[:, s, :, C], k.D[:, columns(i, s)], ACT.Copy)
                act.activation(res[:, s, :, C + 1], k.last[:, columns(i, s)], ACT.Copy).then_inc(side[s], 1)

            def square(i, s):
                act.wait_ge(cent_done[s], i + 1)
                act.wait_ge(ssq_done[s], i)
                act.activation(sq[:, s], cent[:, s], ACT.Square).then_inc(sq_done[s], 1)

            def deviation(i, s):
                act.wait_ge(ssq_done[s], i + 1)
                act.wait_ge(rstd_done[s], i)
                act.activation(std[:, s], ssq[:, s], ACT.Sqrt, bias=k.eps[0:NP, :], scale=1.0 / C
                               ).then_inc(std_done[s], 1)

            if layer:
                staggered(act, (2, deviation), (1, square))
            else:
                staggered(act, (3, deviation), (0, turned), (2, square), (3, beside))

        @block.vector
        def _(dve):
            if not layer:
                dve.memset(zero[:], 0.0).then_inc(zeroed, 1)

            def first_part(i, s):
                dve.wait_ge(loaded[s], i * 64 + 64)
                dve.wait_ge(y_done[s], i)
                if layer:
                    dve.tensor_tensor(pre[:, s], agg[:, s], bc(k.D[:, columns(i, s)], C), ALU.mult
                                      ).then_inc(pre_done[s], 1)
                else:
                    dve.wait_ge(a_done[s], i + 1)
                    dve.tensor_tensor(pre[:, s], ap[s % 2][:], agg[:, s], ALU.add).then_inc(pre_done[s], 1)

            def row(i, s):
                dve.wait_ge(pre_done[s], i + 1)
                dve.wait_ge(cent_done[s], i)
                if layer:
                    dve.scalar_tensor_tensor(y[:, s], xin[:, s, :, 0:C], k.coef[0:NP, 6:7], pre[:, s],
                                             ALU.mult, ALU.add).then_inc(y_done[s], 1)
                else:
                    dve.scalar_tensor_tensor(y[:, s], pre[:, s], 0.0, xin[:, s], ALU.max, ALU.add
                                             ).then_inc(y_done[s], 1)

            def row_sum(i, s):
                dve.wait_ge(y_done[s], i + 1)
                dve.wait_ge(mean_done[s], i)
                dve.tensor_reduce(total[:, s], y[:, s], AX.X, ALU.add).then_inc(sum_done[s], 1)

            def row_mean(i, s):
                dve.wait_ge(sum_done[s], i + 1)
                dve.wait_ge(cent_done[s], i)
                dve.tensor_scalar(mean[:, s], total[:, s], 1.0 / C, None, ALU.mult).then_inc(mean_done[s], 1)

            def squares(i, s):
                dve.wait_ge(sq_done[s], i + 1)
                dve.wait_ge(std_done[s], i)
                if not layer:
                    dve.wait_ge(rsq_done[s], i)
                dve.tensor_reduce(ssq[:, s], sq[:, s], AX.X, ALU.add).then_inc(ssq_done[s], 1)

            def inverse(i, s):
                dve.wait_ge(std_done[s], i + 1)
                dve.wait_ge(res_done[s], i)
                dve.reciprocal(rstd[:, s], std[:, s]).then_inc(rstd_done[s], 1)

            def qsum_factor(i, s):
                dve.wait_ge(rstd_done[s], i + 1)
                dve.tensor_tensor(rsq[:, s], rstd[:, s], rstd[:, s], ALU.mult).then_inc(sum2_done[s], 1)

            def qsum(i, s):
                dve.wait_ge(sum2_done[s], i + 1)
                dve.tensor_tensor(k.qsum[:, columns(i, s)], rsq[:, s], ssq[:, s], ALU.mult).then_inc(rsq_done[s], 1)

            if layer:
                staggered(dve, (0, first_part), (2, inverse), (0, row), (0, row_sum), (0, row_mean), (1, squares))
            else:
                staggered(dve, (0, first_part), (2, inverse), (0, row), (2, qsum_factor), (0, row_sum), (2, qsum),
                          (0, row_mean), (1, squares))

        if not layer:
            @block.tensor
            def _(pe):
                pe.wait_ge(zeroed, 1)
                pe.matmul(k.sums_ps[:], zero[:, 0:1], zero[:], start=True, stop=True)

                def turn(i, s):
                    pe.wait_ge(loaded[s], i * 64 + 64)
                    wait_before(pe, i, s, 1, xT_ready)
                    for j in range(KN // 2):
                        last = pe.transpose(xTp[:, j, 0:NP], xin[:, s, 2 * j:2 * j + 2, :].rearrange("p a c -> p (a c)"),
                                            k.ident[0:NP, 0:NP])
                    last.then_inc(xT_done[s], 1)

                def product(i, s):
                    pe.wait_ge(xT_ready[s], i + 1)
                    wait_before(pe, i, s, 2, pre_done)
                    for j in range(KN // 2):
                        last = pe.matmul(ap[s % 2][:, 2 * j:2 * j + 2, :], xT[:, s % 2, j, 0:NP], k.Wd[:],
                                         start=True, stop=True)
                    last.then_inc(a_done[s], 1)

                def sums(i, s):
                    pe.wait_ge(res_done[s], i + 1)
                    for a in range(0, KN, 8):
                        n = min(8, KN - a)
                        last = pe.matmul(k.sums_ps[:, 0:n * C], k.ones[0:NP, 0:1], res[:, s, a:a + n, 0:C],
                                         start=False, stop=True, skip_group_check=True)
                    last.then_inc(summed[s], 1)

                staggered(pe, (0, turn), (4, sums), (0, product))


def mixing(nc, d, k, scope):
    def sb(nm, shape):
        return scope.enter_context(nc.sbuf_tensor(nm, shape, FP32))

    F = C + 4
    part, csum, feat = sb("c_part", [1, BANK]), sb("c_sum", [1, C]), sb("c_feat", [1, F])
    qs, tiny = sb("c_q", [NP, 1]), sb("c_tiny", [1, 8])
    w1, b1, prod, h = sb("c_w1", [HID, F]), sb("c_b1", [HID, 1]), sb("c_prod", [HID, F]), sb("c_h", [HID, 2])
    w2, b2, lg, cf = sb("c_w2", [HID, NCOEF]), sb("c_b2", [1, NCOEF]), sb("c_lg", [1, 8]), sb("c_cf", [1, 8])
    with ExitStack() as own:
        sem = own.enter_context(semaphores(nc))
        w_in, vch, to_pe, of_pe, to_act, of_act = (sem(x) for x in ("c_w_in", "c_vch", "c_to_pe", "c_of_pe", "c_to_act", "c_of_act"))
        cps = own.enter_context(nc.psum_tensor("c_ps", [P, BANK], FP32))
        block = own.enter_context(nc.Block())
        total = float(N * C)

        @block.sync
        def _(sp):
            sp.dma_start(w1[:], d.W1).then_inc(w_in, 16)
            sp.dma_start(b1[:], d.b1.unsqueeze(1)).then_inc(w_in, 16)
            sp.dma_start(b2[:], d.b2.unsqueeze(0)).then_inc(w_in, 16)
            with nc.allow_non_contiguous_dma(reason="192 weights, turned"):
                sp.dma_start(w2[:], d.W2.rearrange("k h -> h k")).then_inc(w_in, 16)

        @block.vector
        def _(dve):
            link = Chain(dve, vch)
            link(dve.tensor_copy(part[:], k.sums_ps[:]))
            link(dve.tensor_reduce(csum[:], part[:].rearrange("p (a c) -> p c a", c=C), AX.X, ALU.add))
            link(dve.tensor_scalar(feat[:, 0:C], csum[:], 1.0 / N, None, ALU.mult))
            link(dve.tensor_reduce(tiny[:, 0:1], csum[:], AX.X, ALU.add))
            link(dve.tensor_scalar(feat[:, C:C + 1], tiny[:, 0:1], 1.0 / total, None, ALU.mult))
            dve.tensor_reduce(qs[:], k.qsum[:], AX.X, ALU.add).then_inc(to_pe, 1)
            dve.wait_ge(of_pe, 1)
            link(dve.tensor_tensor(tiny[:, 1:2], feat[:, C:C + 1], tiny[:, 0:1], ALU.mult))
            link(dve.tensor_tensor(tiny[:, 2:3], cps[0:1, 0:1], tiny[:, 1:2], ALU.subtract))
            dve.tensor_scalar(tiny[:, 3:4], tiny[:, 2:3], 1.0 / (total - 1), None, ALU.mult).then_inc(to_act, 1)
            dve.memset(feat[:, C + 2:C + 3], float(N))
            link(dve.memset(feat[:, C + 3:C + 4], float(E)))
            dve.wait_ge(of_act, 1)
            dve.sem_inc(to_pe, 1)
            dve.wait_ge(of_pe, 2)
            dve.wait_ge(w_in, 64)
            link(dve.scalar_tensor_tensor(prod[:], w1[:], 1.0, cps[0:HID, 0:F], ALU.mult, ALU.mult,
                                          accum_out=h[:, 0:1]))
            dve.tensor_scalar(h[:, 1:2], h[:, 0:1], b1[:], 0.0, ALU.add, ALU.max).then_inc(to_pe, 1)
            dve.wait_ge(of_pe, 3)
            link(dve.tensor_tensor(lg[:, 0:NCOEF], cps[0:1, 0:NCOEF], b2[:], ALU.add))
            link(dve.tensor_reduce(tiny[:, 4:5], lg[:, 0:NCOEF], AX.X, ALU.max))
            dve.tensor_scalar(lg[:, 0:NCOEF], lg[:, 0:NCOEF], tiny[:, 4:5], None, ALU.subtract).then_inc(to_act, 1)
            dve.wait_ge(of_act, 2)
            link(dve.tensor_reduce(tiny[:, 5:6], cf[:, 0:NCOEF], AX.X, ALU.add))
            link(dve.reciprocal(tiny[:, 6:7], tiny[:, 5:6]))
            link(dve.tensor_scalar(cf[:, 0:NCOEF], cf[:, 0:NCOEF], tiny[:, 6:7], None, ALU.mult))
            link(dve.memset(cf[:, 7:8], 0.0))
            dve.tensor_scalar(cf[:, 6:7], cf[:, 0:1], 1.0, None, ALU.add).then_inc(to_pe, 1)
            dve.wait_ge(of_pe, 4)
            link(dve.tensor_copy(k.coef[:], cps[:, 0:8]))

        @block.scalar
        def _(act):
            act.wait_ge(to_act, 1)
            act.activation(feat[:, C + 1:C + 2], tiny[:, 3:4], ACT.Sqrt).then_inc(of_act, 1)
            act.wait_ge(to_act, 2)
            act.activation(cf[:, 0:NCOEF], lg[:, 0:NCOEF], ACT.Exp).then_inc(of_act, 1)

        @block.tensor
        def _(pe):
            pe.wait_ge(to_pe, 1)
            pe.matmul(cps[0:1, 0:1], qs[:], k.ones[0:NP, 0:1], start=True, stop=True).then_inc(of_pe, 1)
            pe.wait_ge(to_pe, 2)
            pe.matmul(cps[0:HID, 0:F], k.ones[0:1, 0:HID], feat[:], start=True, stop=True).then_inc(of_pe, 1)
            pe.wait_ge(to_pe, 3)
            pe.wait_ge(w_in, 64)
            pe.matmul(cps[0:1, 0:NCOEF], h[:, 1:2], w2[:], start=True, stop=True).then_inc(of_pe, 1)
            pe.wait_ge(to_pe, 4)
            pe.matmul(cps[:, 0:8], k.ones[0:1, 0:P], cf[:], start=True, stop=True).then_inc(of_pe, 1)


_INS = ['x', 'src', 'dst', 'L0_gnn_W', 'L0_gnn_b', 'L1_gnn_W1', 'L1_gnn_b1', 'L1_gnn_W2', 'L1_gnn_b2']


def kernel(**inputs):
    import numpy as _np
    import concourse.bacc as _bacc
    from concourse import mybir as _mybir
    from concourse.bass_utils import run_bass_kernel_spmd as _run

    nc = _bacc.Bacc("TRN2", target_bir_lowering=False, num_devices=1)
    arrays, args = {}, []
    for name in _INS:
        a = _np.ascontiguousarray(inputs[name])
        arrays[f"in_{name}"] = a
        args.append(nc.dram_tensor(f"in_{name}", a.shape, _mybir.dt.from_np(a.dtype), kind="ExternalInput").ap())
    args.append(nc.dram_tensor("out_x", (N, C), _mybir.dt.float32, kind="ExternalOutput").ap())
    build(nc, *args)
    r = _run(nc, [arrays], core_ids=[0])
    return r.results[0]["out_x"]
```

```python
from contextlib import ExitStack, contextmanager

import concourse.bass as bass
from concourse import mybir

FP32, FP16, BF16 = mybir.dt.float32, mybir.dt.float16, mybir.dt.bfloat16
I32, U32, U8 = mybir.dt.int32, mybir.dt.uint32, mybir.dt.uint8
ALU = mybir.AluOpType
ACT = mybir.ActivationFunctionType
AX = mybir.AxisListType
ds = bass.ds

P = 128
N = 100000
C = 64
E = 50000
HID = 32
NCOEF = 6
EPS = 1e-5
NEG = -1e30
ROUND = 12582912.0
FAR = float(1 << 20)

NP = 125
NC = N // NP
NR = NC // 2
NROW = 2 * NP
BANK = 512

ET = 392
EB = ET // 4
EARLY = 3
GT = 4
GPOS = GT * P
NG = 100
NT = NG * GT
NPOS = NG * GPOS
assert E + 2 * GPOS <= NPOS
BLK = 4
ZERO_ROW = NPOS
REC = 408 * P
REC_W = 17
FILLS = 50
FILL_W = N * C // P // FILLS
EXT = C + 2
KN = 10
NCH = NC // KN
NBUF = (4, 5)
SPLIT = (0, 112, NP)


def bc(ap, n):
    return ap.unsqueeze(2).to_broadcast([ap.shape[0], ap.shape[1], n])


@contextmanager
def semaphores(nc):
    held = []

    def sem(name):
        held.append(nc.alloc_semaphore(name))
        return held[-1]

    yield sem
    nc.clear_and_free_semaphores(held)
    nc.all_engine_barrier()


class Names:
    pass


class Chain:

    def __init__(self, eng, sem):
        self.eng, self.sem, self.n = eng, sem, 0

    def __call__(self, instruction):
        instruction.then_inc(self.sem, 1)
        self.n += 1
        self.eng.wait_ge(self.sem, self.n)


def settle(eng, k, *values):
    for v in values:
        eng.lower_val(v)
    eng.wait_ge(k.begun, 1)
    return values


def node_dma(eng, sem, dst, src):
    for a, b in zip(SPLIT, SPLIT[1:]):
        eng.dma_start(dst(a, b), src(a, b)).then_inc(sem, 16)


def build(nc, x, src, dst, W0, b0, W1, b1, W2, b2, out):
    def dram(name, shape, dt):
        return nc.dram_tensor(name, shape, dt).ap()

    d = Names()
    d.x, d.src, d.dst, d.out = x, src, dst, out
    d.W0, d.b0, d.W1, d.b1, d.W2, d.b2 = W0, b0, W1, b1, W2, b2
    d.src_rows = dram("src_rows", [ET * P], FP32)
    d.hi_rows = dram("hi_rows", [ET * P], FP32)
    d.rec = dram("rec", [REC, EXT], FP32)
    d.node_max = dram("node_max", [N, C], FP32)
    d.node_sum = dram("node_sum", [N, C], FP32)
    d.x1 = dram("x1", [N + 1, EXT], FP32)
    d.tab = [dram(f"tab{t}", [NPOS + P, C], FP32) for t in range(2)]
    with ExitStack() as keep:
        def sb(name, shape, dt=FP32):
            return keep.enter_context(nc.sbuf_tensor(name, shape, dt))

        k = Names()
        k.ident, k.upper, k.ones = sb("ident", [P, P]), sb("upper", [P, P]), sb("ones", [P, P])
        k.iota = sb("iota", [P, NR], FP16)
        k.D, k.last, k.qsum = sb("D", [NP, NC]), sb("last", [NP, NC]), sb("qsum", [NP, NC])
        ahead = 2 * GT
        k.dst_at, k.to = sb("dst_at", [P, NT + ahead], U32), sb("to", [P, NT], U32)
        k.last_at, k.w = sb("last_at", [P, NT + ahead], U32), sb("w", [P, NT])
        k.coef, k.eps, k.rounds = sb("coef", [P, 8]), sb("eps", [P, 1]), sb("rounds", [1, 1], I32)
        k.Wd, k.Wb = sb("Wd", [P, P]), sb("Wb", [EXT + 1, 2 * C])
        k.begun = nc.alloc_semaphore("begun")
        count_and_place(nc, d, k)
        with nc.sbuf_tensor("cont", [C, NPOS], U8) as cont:
            k.cont = cont
            edge_pass(nc, d, k, "M", stream=d.rec, scatter=d.node_max)
            with ExitStack() as scope:
                node_pass(nc, d, k, scope, 0)
                mixing(nc, d, k, scope)
            with nc.sbuf_tensor("Xd", [P, NT, C], FP32) as Xd:
                k.Xd = Xd
                edge_pass(nc, d, k, "H5", gather=d.x1, store=d.tab[0], coef=5)
                for step in (4, 3, 2):
                    edge_pass(nc, d, k, f"H{step}", gather=d.tab[step % 2], store=d.tab[1 - step % 2],
                              coef=step, inner=True)
                edge_pass(nc, d, k, "H1", gather=d.tab[1], scatter=d.node_sum, coef=1)
        with ExitStack() as scope:
            node_pass(nc, d, k, scope, 1)


def count_and_place(nc, d, k):
    with ExitStack() as scope:
        def sb(name, shape, dt=FP32):
            return scope.enter_context(nc.sbuf_tensor(name, shape, dt))

        sem = scope.enter_context(semaphores(nc))
        recs = sb("recs", [P, BLK * P, 2])
        hi = sb("hi", [P, 2, BLK * P])
        lo = sb("lo", [P, 2, BLK * P])
        pen = sb("pen", [P, BLK * P])
        mask = sb("mask", [P, GPOS])
        part = sb("part", [P, 2])
        fill = sb("fill", [P, FILL_W])
        edge_x = sb("edge_x", [P, EB, EARLY, C])
        x_at = sb("x_at", [P, ET + 8], U32)
        rec0 = sb("rec0", [P, REC_W, EXT])
        zrow = sb("zrow", [P, C])
        xpad = sb("xpad", [1, EXT])
        wa, wb = sb("wa", [P, C]), sb("wb", [P, C])
        inn = sb("inn", [NP, NC])
        both = sb("both", [NP, NC])
        start = sb("start", [NP, 2, NC])

        init = sem("init")
        fills, rec_filled = sem("fills"), sem("rec_filled")
        const_ready, ids_ready, ids_blank = sem("const_ready"), sem("ids_ready"), sem("ids_blank")
        rows_ready, rows_stored = sem("rows_ready"), sem("rows_stored")
        tr_done, tr_free, keys_ready = sem("tr_done"), sem("tr_free"), sem("keys_ready")
        vch, pch = sem("vch"), sem("pch")
        weights_in, blank_Wb = sem("weights_in"), sem("blank_Wb")

        with (nc.sbuf_tensor("ids", [P, 2, BLK, P], I32) as ids,
              nc.sbuf_tensor("id_rows", [P, 2, BLK, P], FP32) as rows,
              nc.sbuf_tensor("hirow", [P, BLK, P], FP32) as hirow,
              nc.psum_tensor("tr_ps", [P, 4, BANK], FP32) as tr_ps, nc.Block() as block):
            @block.gpsimd
            def _(pool):
                pool.sem_inc(k.begun, 1)
                link = Chain(pool, pch)
                pool.memset(k.Wb[:], 0.0).then_inc(blank_Wb, 1)
                pool.memset(fill[:], NEG).then_inc(init, 1)
                pool.memset(zrow[:], 0.0).then_inc(init, 1)
                link(pool.memset(xpad[:], 0.0))
                pool.memset(xpad[:, C + 1:C + 2], float(ZERO_ROW)).then_inc(init, 1)
                link(pool.memset(k.ident[:], 0.0))
                link(pool.affine_select(out=k.ident[:], in_=k.ident[:], compare_op=ALU.not_equal, fill=1.0,
                                        base=0, pattern=[[-1, P]], channel_multiplier=1))
                link(pool.memset(k.upper[:], 1.0))
                link(pool.affine_select(out=k.upper[:], in_=k.upper[:], compare_op=ALU.is_gt, fill=0.0,
                                        base=0, pattern=[[1, P]], channel_multiplier=-1))
                link(pool.memset(mask[:], 1.0))
                link(pool.affine_select(out=mask[:], in_=mask[:], compare_op=ALU.is_gt, fill=0.0,
                                        base=GPOS - P, pattern=[[-1, GPOS]], channel_multiplier=1))
                pool.iota(part[:], [[-1, 2]], base=0, channel_multiplier=-2, allow_small_or_imprecise_dtypes=True)
                pool.iota(k.iota[:], [[1, NR]], base=0, channel_multiplier=0, allow_small_or_imprecise_dtypes=True)
                pool.memset(k.eps[:], EPS)
                pool.memset(k.ones[:], 1.0).then_inc(const_ready, 1)
                link(pool.memset(k.Wd[:], 0.0))
                pool.wait_ge(weights_in, 7 * 16)
                for h in range(2):
                    a, b = h * C, (h + 1) * C
                    link(pool.tensor_tensor(k.Wd[a:b, a:b], wa[a:b, :], wb[a:b, :], ALU.subtract))

            @block.scalar
            def _(act):
                for h in range(2):
                    act.dma_start(wa[h * C:(h + 1) * C, :], d.W0[0:C, :]).then_inc(weights_in, 16)
                    act.dma_start(wb[h * C:(h + 1) * C, :], d.W0[C:2 * C, :]).then_inc(weights_in, 16)
                act.wait_ge(blank_Wb, 1)
                act.dma_start(k.Wb[0:C, 0:C], d.W0[C:2 * C, :]).then_inc(weights_in, 16)
                act.dma_start(k.Wb[EXT:EXT + 1, 0:C], d.b0.unsqueeze(0)).then_inc(weights_in, 16)
                act.wait_ge(const_ready, 1)
                act.dma_start(k.Wb[EXT - 1:EXT, C:2 * C], k.ones[0:1, 0:C]).then_inc(weights_in, 16)
                act.wait_ge(weights_in, 7 * 16)

            @block.vector
            def _(dve):
                link = Chain(dve, vch)
                dve.memset(ids[:], -1).then_inc(ids_blank, 1)
                link(dve.memset(rec0[:], 0.0))
                dve.memset(rec0[:, :, C:EXT], float(N)).then_inc(init, 1)
                dve.memset(x_at[:, ET:], 0)
                dve.wait_ge(ids_ready, 16 * 10)
                link(dve.tensor_copy(rows[:], ids[:]))
                link(dve.tensor_scalar(hirow[:], rows[:, 0], -(NR - 1) / 2, 1.0 / NR, ALU.add, ALU.mult))
                dve.tensor_scalar(hirow[:], hirow[:], ROUND, ROUND, ALU.add, ALU.subtract).then_inc(rows_ready, 1)
                for which in range(2):
                    dve.wait_ge(tr_done, which + 1)
                    link(dve.tensor_copy(recs[:, :, 1 - which], tr_ps[:, which, :]))
                    v, h, l = recs[:, :, 1 - which], hi[:, which], lo[:, which]
                    link(dve.tensor_scalar(h, v, -(NR - 1) / 2, 1.0 / NR, ALU.add, ALU.mult))
                    link(dve.tensor_scalar(h, h, ROUND, ROUND, ALU.add, ALU.subtract))
                    link(dve.scalar_tensor_tensor(l, h, float(-NR), v, ALU.mult, ALU.add))
                dve.tensor_scalar(x_at[:, 0:ET], recs[:, 0:ET, 0], 0.0, None, ALU.max)
                link(dve.tensor_scalar(pen[:], recs[:, :, 1], 0.0, FAR, ALU.is_lt, ALU.mult))
                dve.tensor_scalar(pen[:], pen[:], 1.0, None, ALU.add).then_inc(keys_ready, 1)

            @block.tensor
            def _(pe):
                pe.wait_ge(const_ready, 1)
                pe.wait_ge(rows_ready, 1)
                for which in range(2):
                    for b in range(BLK):
                        last = pe.transpose(tr_ps[:, which, b * P:(b + 1) * P], rows[:, which, b, :], k.ident[:])
                    last.then_inc(tr_done, 1)

            @block.sync
            def _(sp):
                sp.wait_ge(ids_blank, 1)
                full = E // P
                for which, v in enumerate((d.src, d.dst)):
                    for b in range(BLK - 1):
                        sp.dma_start(ids[:, which, b, :], v[b * P * P:(b + 1) * P * P].rearrange("(t e) -> t e", e=P)
                                     ).then_inc(ids_ready, 16)
                    t = (BLK - 1) * P
                    sp.dma_start(ids[0:full - t, which, BLK - 1, :], v[t * P:full * P].rearrange("(t e) -> t e", e=P)
                                 ).then_inc(ids_ready, 16)
                    sp.dma_start(ids[full - t:full - t + 1, which, BLK - 1, 0:E - full * P],
                                 v[full * P:E].unsqueeze(0)).then_inc(ids_ready, 16)
                sp.wait_ge(rows_ready, 1)
                for tab, rws in ((d.src_rows, rows[:, 0]), (d.hi_rows, hirow[:, :, :])):
                    for b in range(BLK):
                        n = min(P, ET - b * P)
                        sp.dma_start(tab[b * P * P:(b * P + n) * P].rearrange("(t e) -> t e", e=P), rws[0:n, b, :]
                                     ).then_inc(rows_stored, 16)
                sp.wait_ge(rows_stored, 2 * BLK * 16)

        n_fills = 16 * (3 + FILLS)

        oh_ready, oh_used, far_done, dst_ready = (
            [sem(f"{nm}{s}") for s in range(2)] for nm in ("oh_ready", "oh_used", "far_done", "dst_ready"))
        zero_ready, counted, cch = sem("zero_ready"), sem("counted"), sem("cch")
        pref_in, pref_out = sem("pref_in"), sem("pref_out")
        at_ready, gathered, kept = ([sem(f"{nm}{s}") for s in range(2)] for nm in ("at_ready_x", "gathered_x", "kept_x"))
        with ExitStack() as inner:
            isb = lambda name, shape, dt=FP32: inner.enter_context(nc.sbuf_tensor(name, shape, dt))
            ohp = isb("ohp", [P, 2, 4, NROW], BF16)
            ohd = isb("ohd", [P, 2, 4, NROW], BF16)
            ohc = isb("ohc", [P, 2, 4, 2, NR], BF16)
            far = isb("far", [P, 2, 4, NROW])
            zero = isb("zero", [P, BANK], BF16)
            cnt = isb("cnt", [NP, 3, NC])
            at = isb("at_x", [P, 2, EARLY], U32)
            rows_x = isb("rows_x", [P, 2, EARLY, C])
            cum, part1 = isb("cum", [NP, 2, NC]), isb("part1", [NP, 2, NC])
            onesc = isb("onesc", [NP, NC])
            tot = isb("tot", [NP, 2])
            off = isb("off", [NP, 4])
            cps = [inner.enter_context(nc.psum_tensor(f"cps{w}", [NP, 2, BANK], FP32)) for w in range(3)]
            offps = inner.enter_context(nc.psum_tensor("offps", [NP, BANK], FP32))
            block = inner.enter_context(nc.Block())

            @block.vector
            def _(dve):
                dve.memset(zero[:], 0.0).then_inc(zero_ready, 1)
                with dve.Fori(0, EB // 2) as i:
                    for u in range(2):
                        dve.wait_ge(oh_used[u], i)
                        for j in range(4):
                            t = ds(i * 2 + u + j * EB, 1)
                            dve.tensor_scalar(ohp[:, u, j], k.iota[:, 0:NROW], hi[:, 0, t], None, ALU.is_equal)
                            for w in range(2):
                                last = dve.tensor_scalar(ohc[:, u, j, w], k.iota[:], lo[:, w, t], None, ALU.is_equal)
                            last.then_inc(oh_ready[u], 1)
                link = Chain(dve, cch)
                link(dve.memset(onesc[:], 1.0))
                dve.wait_ge(counted, 1)
                for w in range(3):
                    link(dve.tensor_copy(cnt[:, w].rearrange("p (h c) -> p h c", h=2), cps[w][:, :, 0:NR]))
                hs, hd = both[:], cnt[:, 2]
                link(dve.tensor_tensor(hs, cnt[:, 0], cnt[:, 1], ALU.add))
                link(dve.tensor_scalar(inn[:], hd, 0.0, None, ALU.is_gt))
                link(dve.tensor_tensor(part1[:, 0], hs, inn[:], ALU.mult))
                link(dve.tensor_tensor(part1[:, 1], hs, part1[:, 0], ALU.subtract))
                for w in range(2):
                    link(dve.tensor_tensor_scan(cum[:, w], onesc[:], part1[:, w], 0.0, ALU.mult, ALU.add))
                link(dve.tensor_copy(tot[:], cum[:, :, NC - 1]))
                dve.sem_inc(pref_in, 1)
                dve.wait_ge(pref_out, 1)
                link(dve.tensor_copy(off[:], offps[:, 0:4]))
                link(dve.tensor_scalar(off[:, 2:3], off[:, 2:3], 1.0 / (2 * GPOS), 0.5 - 0.5 / (2 * GPOS),
                                       ALU.mult, ALU.add))
                link(dve.tensor_scalar(off[:, 2:3], off[:, 2:3], ROUND, ROUND, ALU.add, ALU.subtract))
                link(dve.tensor_scalar(off[:, 2:3], off[:, 2:3], 1.0, None, ALU.max))
                link(dve.tensor_copy(k.rounds[:], off[0:1, 2:3]))
                link(dve.scalar_tensor_tensor(off[:, 1:2], off[:, 2:3], float(2 * GPOS), off[:, 1:2], ALU.mult, ALU.add))
                for w in range(2):
                    link(dve.scalar_tensor_tensor(cum[:, w], cum[:, w], off[:, w:w + 1], part1[:, w],
                                                  ALU.add, ALU.subtract))
                link(dve.tensor_tensor(cum[:, 0], cum[:, 0], cum[:, 1], ALU.subtract))
                link(dve.tensor_tensor(cum[:, 0], cum[:, 0], inn[:], ALU.mult))
                link(dve.tensor_tensor(start[:, 0], cum[:, 0], cum[:, 1], ALU.add))
                link(dve.tensor_tensor(start[:, 1], start[:, 0], cnt[:, 0], ALU.add))
                dve.tensor_scalar(k.D[:], hd, 1e-12, None, ALU.max).then_inc(pref_in, 1)

            @block.gpsimd
            def _(pool):
                with pool.Fori(0, EB // 2) as i:
                    for s in range(2):
                        again, before = settle(pool, k, i + 1, i)
                        pool.wait_ge(at_ready[s], again)
                        pool.wait_ge(kept[s], before)
                        for j in range(EARLY):
                            pool.indirect_dma_start(
                                out=rows_x[:, s, j, :], out_offset=None, in_=d.x,
                                in_offset=bass.IndirectOffsetOnAxis(ap=at[:, s, j:j + 1], axis=0),
                            ).then_inc(gathered[s], 16)

            @block.scalar
            def _(act):
                def fetch(i, s):
                    act.wait_ge(gathered[s], i * (16 * EARLY))
                    act.activation(at[:, s], x_at[:, ds(i * 8 + s * 4, EARLY)], ACT.Copy).then_inc(at_ready[s], 1)

                def dst_rows(i, u):
                    act.wait_ge(dst_ready[u], i)
                    for j in range(4):
                        last = act.activation(far[:, u, j], k.iota[:, 0:NROW], ACT.Abs, scale=-1.0,
                                              bias=hi[:, 1, ds(i * 2 + u + j * EB, 1)])
                    last.then_inc(far_done[u], 1)
                    act.wait_ge(far_done[u], i + 1)
                    act.wait_ge(oh_used[u], i)
                    act.activation(ohd[:, u], far[:, u], ACT.Relu, bias=1.0, scale=-1.0).then_inc(dst_ready[u], 1)

                for s in range(2):
                    fetch(0, s)
                act.wait_ge(init, 4)
                act.dma_start(d.x1[N:N + 1, :], xpad[:]).then_inc(fills, 16)
                for tab in d.tab:
                    act.dma_start(tab[NPOS:NPOS + P, :], zrow[:]).then_inc(fills, 16)
                with act.Fori(0, EB // 2) as i:
                    for s in range(2):
                        dst_rows(i, s)
                        fetch(i + 1, s)
                        act.activation(edge_x[:, ds(i * 2 + s, 1)].rearrange("p a j c -> p (a j) c"), rows_x[:, s],
                                       ACT.Copy).then_inc(kept[s], 1)
                act.wait_ge(pref_in, 2)
                act.activation(k.D[:], k.D[:], ACT.Sqrt).then_inc(pref_out, 1)

            @block.sync
            def _(sp):
                parts = d.rec.rearrange("(p a r) f -> p a (r f)", p=P, r=REC_W)
                sp.wait_ge(init, 4)
                with sp.Fori(0, REC // P // REC_W) as c:
                    done, = settle(sp, k, c)
                    sp.wait_ge(kept[0], done)
                    sp.dma_start(parts[:, ds(c, 1), :], rec0[:].rearrange("p r f -> p (r f)").unsqueeze(1)
                                 ).then_inc(rec_filled, 16)

            @block.tensor
            def _(pe):
                pe.wait_ge(zero_ready, 1)
                for w in range(3):
                    for h in range(2):
                        pe.matmul(cps[w][:, h, 0:NR], zero[:, 0:NP], zero[:, 0:NR], start=True, stop=True)
                with pe.Fori(0, EB // 2) as i:
                    for u in range(2):
                        pe.wait_ge(dst_ready[u], i + 1)
                        for j in range(4):
                            pe.wait_ge(oh_ready[u], i * 4 + (j + 1))
                            for w, rows in enumerate((ohp, ohd)):
                                for h in range(2):
                                    last = pe.matmul(cps[2 if w else j // 2][:, h, 0:NR], rows[:, u, j, h::2],
                                                     ohc[:, u, j, w], start=False, stop=True, skip_group_check=True)
                        last.then_inc(oh_used[u], 1)
                for u in range(2):
                    pe.wait_ge(oh_used[u], EB // 2)
                pe.sem_inc(counted, 1)
                pe.wait_ge(pref_in, 1)
                pe.matmul(offps[:, 0:2], k.upper[0:NP, 0:NP], tot[:], start=True, stop=True)
                pe.matmul(offps[:, 2:4], k.ones[0:NP, 0:NP], tot[:], start=True, stop=True).then_inc(pref_out, 1)

        two = lambda name: [sem(f"{name}{s}") for s in range(2)]
        rows_in, rows_used, dist_done, hiT_ready = two("rows_in"), two("rows_used"), two("dist_done"), two("hiT_ready")
        onehots, added, table_ready = two("onehots"), two("added"), two("table_ready")
        pos_ready = two("pos_ready")
        got, got_read = [sem(f"got{j}") for j in range(4)], [sem(f"got_read{j}") for j in range(4)]
        rec_ready, scattered, based = two("rec_ready"), two("scattered"), two("based")
        seeded, high_ready, low_left = sem("seeded"), two("high_ready"), two("low_left")
        lch = sem("lch")
        late_at_ready, late_done = two("late_at_ready"), two("late_done")
        with ExitStack() as inner:
            isb = lambda name, shape, dt=FP32: inner.enter_context(nc.sbuf_tensor(name, shape, dt))
            hibc, srcbc = isb("hibc", [P, 2, GPOS]), isb("srcbc", [P, 2, GPOS])
            dist = isb("dist", [NP, 2, GPOS])
            hiT = isb("hiT", [NP, 2, 2, GPOS], BF16)
            ohp = isb("ohp2", [P, 2, 4, NROW], BF16)
            ohc = isb("ohc2", [P, 2, 4, NR], BF16)
            table = isb("table", [NP, 2, 2, 2, NR], BF16)
            eye = isb("eye", [NP, 2, NP], BF16)
            late_at, late_x = isb("late_at", [P, 2, 1], U32), isb("late_x", [P, 2, C])
            eq = isb("eq", [P, 4, GPOS], BF16)
            picked = isb("picked", [P, 4, NR], BF16)
            at, rank, base = isb("at", [P, 2, 4]), isb("rank", [P, 2, 4]), isb("base", [P, 2, 4])
            pos = isb("pos", [P, 2, 4], U32)
            rec = isb("rec_sb", [P, 2, 4, EXT])
            tps = [inner.enter_context(nc.psum_tensor(f"tps{s}", [NP, 2, BANK], FP32)) for s in range(2)]
            gps = [inner.enter_context(nc.psum_tensor(f"gps{j}", [P, BANK], FP32)) for j in range(4)]
            block = inner.enter_context(nc.Block())
            LAST = EB // 2 - 1

            @block.sync
            def _(sp):
                parts = d.node_max.rearrange("r f -> (r f)").rearrange("(p w) -> p w", p=P)
                sp.wait_ge(init, 4)
                for c in range(EB // 2, FILLS):
                    sp.dma_start(parts[:, c * FILL_W:(c + 1) * FILL_W], fill[:]).then_inc(fills, 16)
                with sp.Fori(0, EB // 2) as i:
                    sp.dma_start(parts[:, ds(i * FILL_W, FILL_W)], fill[:]).then_inc(fills, 16)
                    for s in range(2):
                        before, twice = settle(sp, k, i, i * 2)
                        sp.wait_ge(rows_used[s], before)
                        sp.wait_ge(dist_done[s], twice)
                        for to, of in ((hibc, d.hi_rows), (srcbc, d.src_rows)):
                            sp.dma_start(to[:, s], of[ds(i * GPOS + s * (ET // 2 * P), GPOS)].partition_broadcast(P)
                                         ).then_inc(rows_in[s], 16)
                sp.wait_ge(fills, n_fills)

            @block.vector
            def _(dve):
                def ranks(i, s):
                    dve.wait_ge(rows_in[s], i * 32 + 32)
                    for j in range(4):
                        t, n = ds(i * 4 + s * (ET // 2) + j, 1), (j + 1) * P
                        last = dve.scalar_tensor_tensor(eq[:, j, 0:n], srcbc[:, s, 0:n], recs[:, t, 1],
                                                        mask[:, GPOS - n:GPOS], ALU.is_equal, ALU.mult,
                                                        accum_out=rank[:, s, j:j + 1])
                    last.then_inc(rows_used[s], 1)

                def hots(i, s):
                    dve.wait_ge(added[s], i)
                    for j in range(4):
                        t = ds(i * 4 + s * (ET // 2) + j, 1)
                        dve.tensor_scalar(ohp[:, s, j], k.iota[:, 0:NROW], hi[:, 0, t], None, ALU.is_equal)
                        last = dve.tensor_scalar(ohc[:, s, j], k.iota[:], lo[:, 0, t], None, ALU.is_equal)
                    last.then_inc(onehots[s], 1)
                    dve.wait_ge(rows_used[s], i + 1)
                    dve.wait_ge(pos_ready[s], i)
                    dve.tensor_tensor(base[:, s], rank[:, s], pen[:, ds(i * 4 + s * (ET // 2), 4)], ALU.add
                                      ).then_inc(based[s], 1)

                def pick(i, s):
                    dve.wait_ge(onehots[s], i + 1)
                    for j in range(4):
                        dve.wait_ge(got[j], i * 2 + s + 1)
                        dve.scalar_tensor_tensor(picked[:, j], gps[j][:, 0:NR], 1.0, ohc[:, s, j],
                                                 ALU.mult, ALU.mult, accum_out=at[:, s, j:j + 1]
                                                 ).then_inc(got_read[j], 1)

                def positions(i, s):
                    for j in range(4):
                        dve.wait_ge(got_read[j], i * 2 + s + 1)
                    dve.wait_ge(based[s], i + 1)
                    dve.wait_ge(scattered[s], i * 64)
                    dve.tensor_tensor(pos[:, s], at[:, s], base[:, s], ALU.add).then_inc(pos_ready[s], 1)

                def turn(i, s, first=False):
                    ranks(i + s, 1 - s)
                    if not first:
                        positions(i + s - 1, 1 - s)
                    hots(i + s, 1 - s)
                    pick(i, s)

                link = Chain(dve, lch)
                link(dve.tensor_scalar(inn[:], both[:], 0.0, None, ALU.is_gt))
                link(dve.scalar_tensor_tensor(k.last[:], start[:, 0], float(-1 - ZERO_ROW), both[:], ALU.add, ALU.add))
                link(dve.tensor_tensor(k.last[:], k.last[:], inn[:], ALU.mult))
                link(dve.tensor_scalar(k.last[:], k.last[:], float(ZERO_ROW), None, ALU.add))
                ranks(0, 0)
                hots(0, 0)
                turn(0, 0, first=True)
                turn(0, 1)
                with dve.Fori(1, LAST) as i:
                    for s in range(2):
                        turn(i, s)
                turn(LAST, 0)
                positions(LAST, 0)
                pick(LAST, 1)
                positions(LAST, 1)

            @block.tensor
            def _(pe):
                def high_part(s, sign):
                    for h in range(2):
                        last = pe.matmul(tps[s][:, h, 0:NR], eye[:, sign], table[:, s, 0, h],
                                         start=False, stop=True, skip_group_check=True)
                    return last

                for s in range(2):
                    for h in range(2):
                        last = pe.matmul(tps[s][:, h, 0:NR], k.ident[0:NP, 0:NP], start[:, s, h * NR:(h + 1) * NR],
                                         start=True, stop=True)
                last.then_inc(seeded, 1)
                pe.wait_ge(high_ready[0], 1)
                high_part(0, 1).then_inc(low_left[0], 1)
                with pe.Fori(0, EB // 2) as i:
                    for s in range(2):
                        pe.wait_ge(hiT_ready[s], i + 1)
                        pe.wait_ge(table_ready[s], i + 1)
                        for j in range(4):
                            pe.wait_ge(got_read[j], i * 2 + s)
                            for h in range(2):
                                for w in range(2):
                                    last = pe.matmul(gps[j][:, 0:NR], hiT[:, s, h, j * P:(j + 1) * P], table[:, s, w, h],
                                                     start=h + w == 0, stop=h + w == 2)
                            last.then_inc(got[j], 1)
                        high_part(s, 0)
                        pe.wait_ge(high_ready[1 - s], i + s + 1)
                        high_part(1 - s, 1).then_inc(low_left[1 - s], 1)
                        pe.wait_ge(onehots[s], i + 1)
                        for j in range(4):
                            for h in range(2):
                                last = pe.matmul(tps[s][:, h, 0:NR], ohp[:, s, j, h::2], ohc[:, s, j],
                                                 start=False, stop=True, skip_group_check=True)
                        last.then_inc(added[s], 1)

            @block.scalar
            def _(act):
                def rows(i, s):
                    act.wait_ge(rows_in[s], i * 32 + 32)
                    act.wait_ge(hiT_ready[1 - s], i + s)
                    for h in range(2):
                        act.activation(dist[:, h], hibc[0:NP, s], ACT.Abs, bias=part[0:NP, h:h + 1]
                                       ).then_inc(dist_done[s], 1)
                    act.wait_ge(dist_done[s], i * 2 + 2)
                    act.wait_ge(added[s], i)
                    act.activation(hiT[:, s], dist[:], ACT.Relu, bias=1.0, scale=-1.0).then_inc(hiT_ready[s], 1)

                def fetch(i, s):
                    act.wait_ge(late_done[s], i * 16)
                    act.activation(late_at[:, s], x_at[:, ds(i * 4 + s * (ET // 2) + EARLY, 1)], ACT.Copy
                                   ).then_inc(late_at_ready[s], 1)

                def records(i, s):
                    fetch(i + 1, s)
                    act.wait_ge(scattered[s], i * 64)
                    act.activation(rec[:, s, 0:EARLY, 0:C], edge_x[:, ds(i + s * (EB // 2), 1)]
                                   .rearrange("p a j c -> p (a j) c"), ACT.Copy)
                    act.activation(rec[:, s, EARLY, 0:C], late_x[:, s], ACT.Copy)
                    act.activation(rec[:, s, :, C:EXT], recs[:, ds(i * 4 + s * (ET // 2), 4), :], ACT.Copy
                                   ).then_inc(rec_ready[s], 1)

                def high(s, batches):
                    act.wait_ge(added[s], batches)
                    act.activation(table[:, s, 0], tps[s][:, :, 0:NR], ACT.Copy).then_inc(high_ready[s], 1)

                def low(s, batches):
                    act.wait_ge(low_left[s], batches + 1)
                    act.activation(table[:, s, 1], tps[s][:, :, 0:NR], ACT.Copy).then_inc(table_ready[s], 1)

                for sign in range(2):
                    act.activation(eye[:, sign], k.ident[0:NP, 0:NP], ACT.Copy, scale=1.0 - 2.0 * sign)
                for s in range(2):
                    fetch(0, s)
                rows(0, 0)
                act.wait_ge(seeded, 1)
                high(0, 0)
                low(0, 0)
                with act.Fori(0, LAST) as i:
                    for s in range(2):
                        high(1 - s, i + s)
                        records(i, s)
                        rows(i + s, 1 - s)
                        low(1 - s, i + s)
                high(1, LAST)
                records(LAST, 0)
                rows(LAST, 1)
                low(1, LAST)
                high(0, LAST + 1)
                records(LAST, 1)

            @block.gpsimd
            def _(pool):
                pool.wait_ge(rec_filled, REC // P // REC_W * 16)
                def gather(s):
                    pool.indirect_dma_start(
                        out=late_x[:, s, :], out_offset=None, in_=d.x,
                        in_offset=bass.IndirectOffsetOnAxis(ap=late_at[:, s], axis=0),
                    ).then_inc(late_done[s], 16)

                for s in range(2):
                    pool.wait_ge(late_at_ready[s], 1)
                    gather(s)
                with pool.Fori(0, EB // 2) as i:
                    for s in range(2):
                        again, twice = settle(pool, k, i + 1, i + 2)
                        pool.wait_ge(pos_ready[s], again)
                        pool.wait_ge(rec_ready[s], again)
                        for j in range(4):
                            pool.indirect_dma_start(
                                out=d.rec, out_offset=bass.IndirectOffsetOnAxis(ap=pos[:, s, j:j + 1], axis=0),
                                in_=rec[:, s, j, :], in_offset=None, bounds_check=REC - 1, oob_is_err=False,
                            ).then_inc(scattered[s], 16)
                        settle(pool, k)
                        pool.wait_ge(late_at_ready[s], twice)
                        gather(s)
                for s in range(2):
                    pool.wait_ge(scattered[s], EB // 2 * 64)
                    pool.wait_ge(late_done[s], (EB // 2 + 1) * 16)


def edge_pass(nc, d, k, name, gather=None, stream=None, store=None, scatter=None, coef=None, inner=False):
    project, first = stream is not None, coef == 5
    width = EXT if first or project else C
    with ExitStack() as scope:
        def sb(nm, shape, dt=FP32):
            return scope.enter_context(nc.sbuf_tensor(f"{nm}_{name}", shape, dt))

        def ps(nm, shape):
            return [scope.enter_context(nc.psum_tensor(f"{nm}{s}_{name}", shape, FP32)) for s in range(2)]

        sem = scope.enter_context(semaphores(nc))

        def two(nm):
            return [sem(f"{nm}{s}_{name}") for s in range(2)]

        at = sb("at", [P, 2, GT], U32)
        to = sb("to", [P, 2, GT], U32) if scatter is not None else None
        rows = sb("rows", [P, 2, GT, width])
        own = sb("own", [P, 2, GT, C]) if not project and not first else None
        z = sb("z", [P, 2, GT, C]) if not project else rows
        sums = sb("sums", [C, 2, GPOS])
        back = sb("back", [P, 2, GT, C])
        zT = ps("zT", [EXT if project else C, BANK])
        backT = ps("backT", [P, BANK])
        if project:
            zeros = sb("zeros", [P, FILL_W])
            fills, zeros_set = sem("fills_M"), sem("zeros_set")
            xT = sb("xT", [EXT + 1, 2, GPOS])
            pen = sb("pen", [C, 2, GPOS])
            behind = sb("behind", [P, 2, GT, 2])
            goes_on = sb("goes_on", [P, 2, GT])
            srcs = sb("srcs", [P, 2, GPOS + 1])
            vT = ps("vT", [2 * C, BANK])
            xT_ready, pen_ready, vT_done = two("xT_ready"), two("pen_ready"), two("vT_done")
            compared, ids_kept, marked = two("compared"), two("ids_kept"), two("marked")
            srcs_ready = two("srcs_ready")
        at_ready, gathered = two("at_ready"), two("gathered")
        own_ready, z_ready, zT_done = two("own_ready"), two("z_ready"), two("zT_done")
        scanned, backT_done, back_ready = two("scanned"), two("backT_done"), two("back_ready")
        away = two("away")
        begun, ich = (sem(f"{nm}_{name}") for nm in ("begun", "ich"))
        at_table = k.dst_at if first else k.last_at
        LAST = NG // 2 - 1

        block = scope.enter_context(nc.Block())

        def rounds(eng):
            return eng.value_load(k.rounds[0:1, 0:1], min_val=1, max_val=NG // 2) if inner else NG // 2

        @block.gpsimd
        def _(pool):
            def gather_group(i, s):
                again, = settle(pool, k, i + 1)
                pool.wait_ge(at_ready[s], again)
                pool.wait_ge(z_ready[s], i)
                for j in range(GT):
                    pool.indirect_dma_start(
                        out=rows[:, s, j, :], out_offset=None, in_=gather,
                        in_offset=bass.IndirectOffsetOnAxis(ap=at[:, s, j:j + 1], axis=0),
                    ).then_inc(gathered[s], 16)

            def scatter_group(i, s):
                again, = settle(pool, k, i + 1)
                pool.wait_ge(back_ready[s], again)
                for j in range(GT):
                    pool.indirect_dma_start(
                        out=scatter, out_offset=bass.IndirectOffsetOnAxis(ap=to[:, s, j:j + 1], axis=0),
                        in_=back[:, s, j, :], in_offset=None, bounds_check=N - 1, oob_is_err=False,
                    ).then_inc(away[s], 16)

            if project:
                with pool.Fori(0, NG // 2) as i:
                    for s in range(2):
                        scatter_group(i, s)
            elif scatter is None:
                with pool.Fori(0, rounds(pool)) as i:
                    for s in range(2):
                        gather_group(i, s)
            else:
                for s in range(2):
                    gather_group(0, s)
                with pool.Fori(1, NG // 2) as i:
                    for s in range(2):
                        gather_group(i, s)
                        scatter_group(i - 1, s)
                for s in range(2):
                    scatter_group(NG // 2 - 1, s)
            if scatter is not None:
                for s in range(2):
                    pool.wait_ge(away[s], NG // 2 * GT * 16)

        @block.sync
        def _(sp):
            if project:
                sp.wait_ge(zeros_set, 1)
                parts = d.node_sum.rearrange("r f -> (r f)").rearrange("(p w) -> p w", p=P)
                with sp.Fori(0, NG // 2) as i:
                    sp.dma_start(parts[:, ds(i * FILL_W, FILL_W)], zeros[:]).then_inc(fills, 16)
                    sp.dma_start(d.tab[1][ds(i * (2 * GPOS), 2 * GPOS), :].rearrange("(p r) f -> p (r f)", p=P),
                                 zeros[:, 0:2 * GPOS * C // P]).then_inc(fills, 16)
                    for s in range(2):
                        before, = settle(sp, k, i)
                        sp.wait_ge(zT_done[s], before)
                        sp.wait_ge(ids_kept[s], before)
                        sp.dma_start(rows[:, s], stream[ds(i * (2 * GPOS) + s * GPOS + 1, GPOS), :]
                                     .rearrange("(j p) f -> p j f", p=P)).then_inc(gathered[s], 16)
                        with nc.allow_non_contiguous_dma(reason="two ids of each record"):
                            sp.dma_start(behind[:, s], stream[ds(i * (2 * GPOS) + s * GPOS + 2, GPOS), C:EXT]
                                         .rearrange("(j p) f -> p j f", p=P)).then_inc(gathered[s], 16)
                sp.wait_ge(fills, NG // 2 * 32)
            if store is not None:
                n = rounds(sp)
                with sp.Fori(0, n) as i:
                    for s in range(2):
                        sp.wait_ge(back_ready[s], i + 1)
                        sp.dma_start(store[ds(i * (2 * GPOS) + s * GPOS, GPOS), :].rearrange("(j p) f -> p j f", p=P),
                                     back[:, s]).then_inc(away[s], 16)
                landed, = settle(sp, k, n * 16)
                for s in range(2):
                    sp.wait_ge(away[s], landed)

        @block.scalar
        def _(act):
            def fetch(i, s):
                act.wait_ge(gathered[s], i * (GT * 16))
                act.activation(at[:, s], at_table[:, ds(i * (2 * GT) + s * GT, GT)], ACT.Copy
                               ).then_inc(at_ready[s], 1)

            def prepare(i, s):
                if not first:
                    act.wait_ge(z_ready[s], i)
                    act.activation(own[:, s], k.Xd[:, ds(i * (2 * GT) + s * GT, GT), :], ACT.Copy,
                                   scale=k.coef[:, coef:coef + 1]).then_inc(own_ready[s], 1)

            def turned(i, s):
                act.wait_ge(zT_done[s], i + 1)
                act.wait_ge(vT_done[s], i)
                act.activation(xT[0:EXT, s], zT[s][:], ACT.Copy).then_inc(xT_ready[s], 1)

            def source(i, s):
                act.wait_ge(vT_done[s], i + 1)
                act.wait_ge(marked[s], i)
                act.wait_ge(srcs_ready[1 - s], i + s)
                act.activation(srcs[C:2 * C, s, 0:1], srcs[C:2 * C, 1 - s, GPOS:], ACT.Copy)
                act.activation(srcs[C:2 * C, s, 1:], vT[s][C:2 * C, :], ACT.Copy).then_inc(srcs_ready[s], 1)

            def give_back(i, s):
                act.wait_ge(backT_done[s], i + 1)
                act.wait_ge(away[s], i * (16 if scatter is None else 16 * GT))
                if project:
                    act.wait_ge(ids_kept[s], i + 1)
                if scatter is not None:
                    act.activation(to[:, s], k.to[:, ds(i * (2 * GT) + s * GT, GT)], ACT.Copy)
                act.activation(back[:, s].rearrange("p j c -> p (j c)"), backT[s][:, 0:GT * C], ACT.Copy
                               ).then_inc(back_ready[s], 1)

            if project:
                act.wait_ge(begun, 1)
                turned(0, 0)
                source(0, 0)
                with act.Fori(0, LAST) as i:
                    for s in range(2):
                        turned(i + s, 1 - s)
                        source(i + s, 1 - s)
                        give_back(i, s)
                turned(LAST, 1)
                source(LAST, 1)
                for s in range(2):
                    give_back(LAST, s)
                return
            n = rounds(act)
            for s in range(2):
                fetch(0, s)
            with act.Fori(0, n) as i:
                prepare(i, 0)
                fetch(i + 1, 0)
                prepare(i, 1)
                give_back(i, 0)
                fetch(i + 1, 1)
                give_back(i, 1)

        @block.vector
        def _(dve):
            n = rounds(dve)
            if project:
                dve.memset(zeros[:], 0.0).then_inc(zeros_set, 1)
                dve.memset(srcs[C:2 * C, 1, GPOS:], -2.0)
                dve.memset(xT[C:EXT + 1, :, :], 1.0).then_inc(begun, 1)
                dve.memset(k.dst_at[:, NT:], 0)
                dve.memset(k.last_at[:, NT:], 0)
            dve.memset(sums[:, 1, GPOS - 1:GPOS], 0.0).then_inc(ich, 1)
            dve.wait_ge(ich, 1)
            with dve.Fori(0, n) as i:
                for s in range(2):
                    tiles = ds(i * (2 * GT) + s * GT, GT)
                    if project:
                        dve.wait_ge(gathered[s], i * 32 + 32)
                        dve.tensor_tensor(goes_on[:, s], rows[:, s, :, C + 1], behind[:, s, :, 1], ALU.is_equal
                                          ).then_inc(compared[s], 1)
                        dve.tensor_copy(k.dst_at[:, tiles], rows[:, s, :, C])
                        dve.wait_ge(compared[s], i + 1)
                        dve.scalar_tensor_tensor(k.to[:, tiles], goes_on[:, s], FAR, rows[:, s, :, C + 1],
                                                 ALU.mult, ALU.add).then_inc(ids_kept[s], 1)
                        dve.wait_ge(ids_kept[s], i + 1)
                    else:
                        dve.wait_ge(gathered[s], i * (GT * 16) + GT * 16)
                        dve.wait_ge(zT_done[s], i)
                    if first:
                        last_D = rows[:, s, :, C]
                        dve.tensor_copy(k.last_at[:, tiles], rows[:, s, :, C + 1])
                        dve.tensor_tensor(k.w[:, tiles], last_D, last_D, ALU.mult)
                        for j in range(GT):
                            D = rows[:, s, j, C:C + 1]
                            dve.tensor_scalar(k.Xd[:, ds(i * (2 * GT) + s * GT + j, 1), :].rearrange("p a c -> p (a c)"),
                                              rows[:, s, j, 0:C], D, None, ALU.mult)
                            last = dve.tensor_scalar(z[:, s, j], rows[:, s, j, 0:C], D, k.coef[:, 5:6],
                                                     ALU.mult, ALU.mult)
                        last.then_inc(z_ready[s], 1)
                    elif not project:
                        dve.wait_ge(own_ready[s], i + 1)
                        for j in range(GT):
                            last = dve.scalar_tensor_tensor(z[:, s, j], rows[:, s, j],
                                                            k.w[:, ds(i * (2 * GT) + s * GT + j, 1)],
                                                            own[:, s, j], ALU.mult, ALU.add)
                        last.then_inc(z_ready[s], 1)
                    dve.wait_ge((vT_done if project else zT_done)[s], i + 1)
                    dve.wait_ge(backT_done[s], i)
                    dve.wait_ge(scanned[1 - s], i + s)
                    state = sums[:, 1 - s, GPOS - 1:GPOS]
                    cont = k.cont[:, ds(i * (2 * GPOS) + s * GPOS, GPOS)]
                    if project:
                        dve.wait_ge(srcs_ready[s], i + 1)
                        dve.tensor_tensor(cont, srcs[C:2 * C, s, 1:], srcs[C:2 * C, s, 0:GPOS], ALU.is_equal
                                          ).then_inc(marked[s], 1)
                        dve.wait_ge(marked[s], i + 1)
                        dve.tensor_scalar(pen[:, s], cont, 1.0, -NEG, ALU.subtract, ALU.mult).then_inc(pen_ready[s], 1)
                        dve.wait_ge(pen_ready[s], i + 1)
                        dve.tensor_tensor_scan(sums[:, s], pen[:, s], vT[s][0:C, :], state, ALU.add, ALU.max
                                               ).then_inc(scanned[s], 1)
                    else:
                        dve.tensor_tensor_scan(sums[:, s], cont, zT[s][:], state, ALU.mult, ALU.add
                                               ).then_inc(scanned[s], 1)
            if project:
                dve.reciprocal(k.D[:], k.D[:])

        @block.tensor
        def _(pe):
            def turn(i, s):
                again, rows_in = settle(pe, k, i + 1, i * 32 + 32)
                if project:
                    pe.wait_ge(gathered[s], rows_in)
                    pe.wait_ge(xT_ready[s], i)
                else:
                    pe.wait_ge(z_ready[s], again)
                    pe.wait_ge(scanned[s], i)
                for j in range(GT):
                    last = pe.transpose(zT[s][:, j * P:(j + 1) * P], z[:, s, j, 0:EXT if project else C], k.ident[:])
                last.then_inc(zT_done[s], 1)

            def product(i, s):
                pe.wait_ge(xT_ready[s], i + 1)
                pe.wait_ge(scanned[s], i)
                pe.matmul(vT[s][:], k.Wb[:], xT[:, s], start=True, stop=True).then_inc(vT_done[s], 1)

            def turn_back(i, s):
                again, = settle(pe, k, i + 1)
                pe.wait_ge(scanned[s], again)
                pe.wait_ge(back_ready[s], i)
                for j in range(GT):
                    last = pe.transpose(backT[s][:, j * C:(j + 1) * C], sums[:, s, j * P:(j + 1) * P],
                                        k.ident[0:C, 0:C])
                last.then_inc(backT_done[s], 1)

            if project:
                pe.wait_ge(begun, 1)
                turn(0, 0)
                product(0, 0)
                with pe.Fori(0, LAST) as i:
                    for s in range(2):
                        turn(i + s, 1 - s)
                        product(i + s, 1 - s)
                        turn_back(i, s)
                turn(LAST, 1)
                product(LAST, 1)
                turn_back(LAST, 0)
                turn_back(LAST, 1)
                return
            with pe.Fori(0, rounds(pe)) as i:
                for s in range(2):
                    turn(i, s)
                    turn_back(i, s)


def node_pass(nc, d, k, scope, layer):
    def sb(nm, shape, dt=FP32):
        return scope.enter_context(nc.sbuf_tensor(f"{nm}_n{layer}", shape, dt))

    def ps(nm, shape):
        return scope.enter_context(nc.psum_tensor(f"{nm}_n{layer}", shape, FP32))

    wide = EXT if layer else C
    nbuf = NBUF[layer]
    xin = sb("xin", [NP, nbuf, KN, wide])
    agg = sb("agg", [NP, nbuf, KN, C])
    pre, y, cent, sq = (sb(nm, [NP, nbuf, KN, C]) for nm in ("pre", "y", "cent", "sq"))
    res = sb("res", [NP, nbuf, KN, C if layer else EXT])
    total, mean, ssq, std, rstd, rsq = (
        sb(nm, [NP, nbuf, KN]) for nm in ("total", "mean", "ssq", "std", "rstd", "rsq"))
    table = (d.x1[0:N, :] if layer else d.x).rearrange("(p c) f -> p c f", c=NC)
    edges = (d.node_sum if layer else d.node_max).rearrange("(p c) f -> p c f", c=NC)
    target = (d.out if layer else d.x1[0:N, :]).rearrange("(p c) f -> p c f", c=NC)
    if not layer:
        xT = sb("xT", [P, 2, KN // 2, P])
        xTp = ps("xTp", [P, KN // 2, P])
        ap = [ps(f"ap{s}", [NP, KN, C]) for s in range(2)]
        k.sums_ps = ps("sums", [1, BANK])
        zero = sb("zero", [P, BANK], BF16)

    with ExitStack() as sems:
        sem = sems.enter_context(semaphores(nc))
        (loaded, pre_done, y_done, sum_done, mean_done, cent_done, sq_done, ssq_done, std_done, rstd_done, rsq_done,
         res_done, side, stored, xT_done, xT_ready, a_done, summed) = (
            [sem(f"{nm}{s}_n{layer}") for s in range(nbuf)] for nm in (
                "loaded", "pre_done", "y_done", "sum_done", "mean_done", "cent_done", "sq_done", "ssq_done", "std_done",
                "rstd_done", "rsq_done", "res_done", "side", "stored", "xT_done", "xT_ready", "a_done", "summed"))
        zeroed = sem(f"zeroed_n{layer}")
        sum2_done = [sem(f"sum2_done{s}_n{layer}") for s in range(nbuf)]
        block = sems.enter_context(nc.Block())

        def columns(i, s):
            return ds(i * (nbuf * KN) + s * KN, KN)

        def staggered(eng, *steps):
            most = max(lag for lag, _ in steps)
            assert most <= nbuf

            def turn(i, s):
                for lag, step in steps:
                    if isinstance(i, int) and not 0 <= nbuf * i + s - lag < NCH:
                        continue
                    step(i, s - lag) if s >= lag else step(i - 1, s - lag + nbuf)

            for s in range(nbuf):
                turn(0, s)
            with eng.Fori(1, NCH // nbuf) as i:
                for s in range(nbuf):
                    turn(i, s)
            for s in range(most):
                turn(NCH // nbuf, s)

        def before(i, s, n, sems):
            if s >= n:
                return sems[s - n], i + 1
            if isinstance(i, int) and i == 0:
                return None
            return sems[s - n + nbuf], i

        def wait_before(eng, i, s, n, sems):
            found = before(i, s, n, sems)
            if found:
                eng.wait_ge(*found)

        def store(eng, i, s):
            cols = columns(i, s)
            eng.wait_ge(res_done[s], i + 1)
            if not layer:
                eng.wait_ge(side[s], i + 1)
            node_dma(eng, stored[s], lambda a, b: target[a:b, cols, :], lambda a, b: res[a:b, s])

        @block.sync
        def _(sp):
            def load(i, s):
                cols = columns(i, s)
                sp.wait_ge(y_done[s], i)
                if not layer:
                    sp.wait_ge(xT_done[s], i)
                node_dma(sp, loaded[s], lambda a, b: xin[a:b, s], lambda a, b: table[a:b, cols, :])
                node_dma(sp, loaded[s], lambda a, b: agg[a:b, s], lambda a, b: edges[a:b, cols, :])

            if layer:
                staggered(sp, (0, load))
            else:
                staggered(sp, (0, load), (4, lambda i, s: store(sp, i, s)))
                for s in range(nbuf):
                    sp.wait_ge(stored[s], NCH // nbuf * 32)

        @block.gpsimd
        def _(pool):
            def centre(i, s):
                pool.wait_ge(mean_done[s], i + 1)
                pool.wait_ge(res_done[s], i)
                pool.wait_ge(sq_done[s], i)
                pool.tensor_tensor(cent[:, s], y[:, s], bc(mean[:, s], C), ALU.subtract).then_inc(cent_done[s], 1)

            def scale(i, s):
                pool.wait_ge(cent_done[s], i + 1)
                pool.wait_ge(rstd_done[s], i + 1)
                pool.wait_ge(stored[s], i * 32)
                if not layer:
                    pool.wait_ge(summed[s], i)
                pool.tensor_tensor(res[:, s, :, 0:C], cent[:, s], bc(rstd[:, s], C), ALU.mult).then_inc(res_done[s], 1)

            staggered(pool, (2, scale), (0, centre))

        @block.scalar
        def _(act):
            def turned(i, s):
                act.wait_ge(xT_done[s], i + 1)
                wait_before(act, i, s, 2, a_done)
                act.activation(xT[:, s % 2, :, 0:NP], xTp[:, :, 0:NP], ACT.Copy).then_inc(xT_ready[s], 1)

            def beside(i, s):
                act.wait_ge(stored[s], i * 32)
                act.activation(res[:, s, :, C], k.D[:, columns(i, s)], ACT.Copy)
                act.activation(res[:, s, :, C + 1], k.last[:, columns(i, s)], ACT.Copy).then_inc(side[s], 1)

            def square(i, s):
                act.wait_ge(cent_done[s], i + 1)
                act.wait_ge(ssq_done[s], i)
                act.activation(sq[:, s], cent[:, s], ACT.Square).then_inc(sq_done[s], 1)

            def deviation(i, s):
                act.wait_ge(ssq_done[s], i + 1)
                act.wait_ge(rstd_done[s], i)
                act.activation(std[:, s], ssq[:, s], ACT.Sqrt, bias=k.eps[0:NP, :], scale=1.0 / C
                               ).then_inc(std_done[s], 1)

            if layer:
                staggered(act, (3, deviation), (2, square), (5, lambda i, s: store(act, i, s)))
                for s in range(nbuf):
                    act.wait_ge(stored[s], NCH // nbuf * 32)
            else:
                staggered(act, (3, deviation), (0, turned), (2, square), (3, beside))

        @block.vector
        def _(dve):
            if not layer:
                dve.memset(zero[:], 0.0).then_inc(zeroed, 1)

            def first_part(i, s):
                dve.wait_ge(loaded[s], i * 64 + 64)
                dve.wait_ge(y_done[s], i)
                if layer:
                    dve.tensor_tensor(pre[:, s], agg[:, s], bc(k.D[:, columns(i, s)], C), ALU.mult
                                      ).then_inc(pre_done[s], 1)
                else:
                    dve.wait_ge(a_done[s], i + 1)
                    dve.tensor_tensor(pre[:, s], ap[s % 2][:], agg[:, s], ALU.add).then_inc(pre_done[s], 1)

            def row(i, s):
                dve.wait_ge(pre_done[s], i + 1)
                dve.wait_ge(cent_done[s], i)
                if layer:
                    dve.scalar_tensor_tensor(y[:, s], xin[:, s, :, 0:C], k.coef[0:NP, 6:7], pre[:, s],
                                             ALU.mult, ALU.add).then_inc(y_done[s], 1)
                else:
                    dve.scalar_tensor_tensor(y[:, s], pre[:, s], 0.0, xin[:, s], ALU.max, ALU.add
                                             ).then_inc(y_done[s], 1)

            def row_sum(i, s):
                dve.wait_ge(y_done[s], i + 1)
                dve.wait_ge(mean_done[s], i)
                dve.tensor_reduce(total[:, s], y[:, s], AX.X, ALU.add).then_inc(sum_done[s], 1)

            def row_mean(i, s):
                dve.wait_ge(sum_done[s], i + 1)
                dve.wait_ge(cent_done[s], i)
                dve.tensor_scalar(mean[:, s], total[:, s], 1.0 / C, None, ALU.mult).then_inc(mean_done[s], 1)

            def squares(i, s):
                dve.wait_ge(sq_done[s], i + 1)
                dve.wait_ge(std_done[s], i)
                if not layer:
                    dve.wait_ge(rsq_done[s], i)
                dve.tensor_reduce(ssq[:, s], sq[:, s], AX.X, ALU.add).then_inc(ssq_done[s], 1)

            def inverse(i, s):
                dve.wait_ge(std_done[s], i + 1)
                dve.wait_ge(res_done[s], i)
                dve.reciprocal(rstd[:, s], std[:, s]).then_inc(rstd_done[s], 1)

            def qsum_factor(i, s):
                dve.wait_ge(rstd_done[s], i + 1)
                dve.tensor_tensor(rsq[:, s], rstd[:, s], rstd[:, s], ALU.mult).then_inc(sum2_done[s], 1)

            def qsum(i, s):
                dve.wait_ge(sum2_done[s], i + 1)
                dve.tensor_tensor(k.qsum[:, columns(i, s)], rsq[:, s], ssq[:, s], ALU.mult).then_inc(rsq_done[s], 1)

            if layer:
                staggered(dve, (1, row), (0, first_part), (1, row_sum), (3, inverse), (1, row_mean), (2, squares))
            else:
                staggered(dve, (0, first_part), (2, inverse), (0, row), (2, qsum_factor), (0, row_sum), (2, qsum),
                          (0, row_mean), (1, squares))

        if not layer:
            @block.tensor
            def _(pe):
                pe.wait_ge(zeroed, 1)
                pe.matmul(k.sums_ps[:], zero[:, 0:1], zero[:], start=True, stop=True)

                def turn(i, s):
                    pe.wait_ge(loaded[s], i * 64 + 64)
                    wait_before(pe, i, s, 1, xT_ready)
                    for j in range(KN // 2):
                        last = pe.transpose(xTp[:, j, 0:NP], xin[:, s, 2 * j:2 * j + 2, :].rearrange("p a c -> p (a c)"),
                                            k.ident[0:NP, 0:NP])
                    last.then_inc(xT_done[s], 1)

                def product(i, s):
                    pe.wait_ge(xT_ready[s], i + 1)
                    wait_before(pe, i, s, 2, pre_done)
                    for j in range(KN // 2):
                        last = pe.matmul(ap[s % 2][:, 2 * j:2 * j + 2, :], xT[:, s % 2, j, 0:NP], k.Wd[:],
                                         start=True, stop=True)
                    last.then_inc(a_done[s], 1)

                def sums(i, s):
                    pe.wait_ge(res_done[s], i + 1)
                    for a in range(0, KN, 8):
                        n = min(8, KN - a)
                        last = pe.matmul(k.sums_ps[:, 0:n * C], k.ones[0:NP, 0:1], res[:, s, a:a + n, 0:C],
                                         start=False, stop=True, skip_group_check=True)
                    last.then_inc(summed[s], 1)

                staggered(pe, (0, turn), (4, sums), (0, product))


def mixing(nc, d, k, scope):
    def sb(nm, shape):
        return scope.enter_context(nc.sbuf_tensor(nm, shape, FP32))

    F = C + 4
    part, csum, feat = sb("c_part", [1, BANK]), sb("c_sum", [1, C]), sb("c_feat", [1, F])
    qs, tiny = sb("c_q", [NP, 1]), sb("c_tiny", [1, 8])
    w1, b1, prod, h = sb("c_w1", [HID, F]), sb("c_b1", [HID, 1]), sb("c_prod", [HID, F]), sb("c_h", [HID, 2])
    w2, b2, lg, cf = sb("c_w2", [HID, NCOEF]), sb("c_b2", [1, NCOEF]), sb("c_lg", [1, 8]), sb("c_cf", [1, 8])
    with ExitStack() as own:
        sem = own.enter_context(semaphores(nc))
        w_in, vch, to_pe, of_pe, to_act, of_act = (sem(x) for x in ("c_w_in", "c_vch", "c_to_pe", "c_of_pe", "c_to_act", "c_of_act"))
        cps = own.enter_context(nc.psum_tensor("c_ps", [P, BANK], FP32))
        block = own.enter_context(nc.Block())
        total = float(N * C)

        @block.sync
        def _(sp):
            sp.dma_start(w1[:], d.W1).then_inc(w_in, 16)
            sp.dma_start(b1[:], d.b1.unsqueeze(1)).then_inc(w_in, 16)
            sp.dma_start(b2[:], d.b2.unsqueeze(0)).then_inc(w_in, 16)
            with nc.allow_non_contiguous_dma(reason="192 weights, turned"):
                sp.dma_start(w2[:], d.W2.rearrange("k h -> h k")).then_inc(w_in, 16)

        @block.vector
        def _(dve):
            link = Chain(dve, vch)
            link(dve.tensor_copy(part[:], k.sums_ps[:]))
            link(dve.tensor_reduce(csum[:], part[:].rearrange("p (a c) -> p c a", c=C), AX.X, ALU.add))
            link(dve.tensor_scalar(feat[:, 0:C], csum[:], 1.0 / N, None, ALU.mult))
            link(dve.tensor_reduce(tiny[:, 0:1], csum[:], AX.X, ALU.add))
            link(dve.tensor_scalar(feat[:, C:C + 1], tiny[:, 0:1], 1.0 / total, None, ALU.mult))
            dve.tensor_reduce(qs[:], k.qsum[:], AX.X, ALU.add).then_inc(to_pe, 1)
            dve.wait_ge(of_pe, 1)
            link(dve.tensor_tensor(tiny[:, 1:2], feat[:, C:C + 1], tiny[:, 0:1], ALU.mult))
            link(dve.tensor_tensor(tiny[:, 2:3], cps[0:1, 0:1], tiny[:, 1:2], ALU.subtract))
            dve.tensor_scalar(tiny[:, 3:4], tiny[:, 2:3], 1.0 / (total - 1), None, ALU.mult).then_inc(to_act, 1)
            dve.memset(feat[:, C + 2:C + 3], float(N))
            link(dve.memset(feat[:, C + 3:C + 4], float(E)))
            dve.wait_ge(of_act, 1)
            dve.sem_inc(to_pe, 1)
            dve.wait_ge(of_pe, 2)
            dve.wait_ge(w_in, 64)
            link(dve.scalar_tensor_tensor(prod[:], w1[:], 1.0, cps[0:HID, 0:F], ALU.mult, ALU.mult,
                                          accum_out=h[:, 0:1]))
            dve.tensor_scalar(h[:, 1:2], h[:, 0:1], b1[:], 0.0, ALU.add, ALU.max).then_inc(to_pe, 1)
            dve.wait_ge(of_pe, 3)
            link(dve.tensor_tensor(lg[:, 0:NCOEF], cps[0:1, 0:NCOEF], b2[:], ALU.add))
            link(dve.tensor_reduce(tiny[:, 4:5], lg[:, 0:NCOEF], AX.X, ALU.max))
            dve.tensor_scalar(lg[:, 0:NCOEF], lg[:, 0:NCOEF], tiny[:, 4:5], None, ALU.subtract).then_inc(to_act, 1)
            dve.wait_ge(of_act, 2)
            link(dve.tensor_reduce(tiny[:, 5:6], cf[:, 0:NCOEF], AX.X, ALU.add))
            link(dve.reciprocal(tiny[:, 6:7], tiny[:, 5:6]))
            link(dve.tensor_scalar(cf[:, 0:NCOEF], cf[:, 0:NCOEF], tiny[:, 6:7], None, ALU.mult))
            link(dve.memset(cf[:, 7:8], 0.0))
            dve.tensor_scalar(cf[:, 6:7], cf[:, 0:1], 1.0, None, ALU.add).then_inc(to_pe, 1)
            dve.wait_ge(of_pe, 4)
            link(dve.tensor_copy(k.coef[:], cps[:, 0:8]))

        @block.scalar
        def _(act):
            act.wait_ge(to_act, 1)
            act.activation(feat[:, C + 1:C + 2], tiny[:, 3:4], ACT.Sqrt).then_inc(of_act, 1)
            act.wait_ge(to_act, 2)
            act.activation(cf[:, 0:NCOEF], lg[:, 0:NCOEF], ACT.Exp).then_inc(of_act, 1)

        @block.tensor
        def _(pe):
            pe.wait_ge(to_pe, 1)
            pe.matmul(cps[0:1, 0:1], qs[:], k.ones[0:NP, 0:1], start=True, stop=True).then_inc(of_pe, 1)
            pe.wait_ge(to_pe, 2)
            pe.matmul(cps[0:HID, 0:F], k.ones[0:1, 0:HID], feat[:], start=True, stop=True).then_inc(of_pe, 1)
            pe.wait_ge(to_pe, 3)
            pe.wait_ge(w_in, 64)
            pe.matmul(cps[0:1, 0:NCOEF], h[:, 1:2], w2[:], start=True, stop=True).then_inc(of_pe, 1)
            pe.wait_ge(to_pe, 4)
            pe.matmul(cps[:, 0:8], k.ones[0:1, 0:P], cf[:], start=True, stop=True).then_inc(of_pe, 1)


_INS = ['x', 'src', 'dst', 'L0_gnn_W', 'L0_gnn_b', 'L1_gnn_W1', 'L1_gnn_b1', 'L1_gnn_W2', 'L1_gnn_b2']


def kernel(**inputs):
    import numpy as _np
    import concourse.bacc as _bacc
    from concourse import mybir as _mybir
    from concourse.bass_utils import run_bass_kernel_spmd as _run

    nc = _bacc.Bacc("TRN2", target_bir_lowering=False, num_devices=1)
    arrays, args = {}, []
    for name in _INS:
        a = _np.ascontiguousarray(inputs[name])
        arrays[f"in_{name}"] = a
        args.append(nc.dram_tensor(f"in_{name}", a.shape, _mybir.dt.from_np(a.dtype), kind="ExternalInput").ap())
    args.append(nc.dram_tensor("out_x", (N, C), _mybir.dt.float32, kind="ExternalOutput").ap())
    build(nc, *args)
    r = _run(nc, [arrays], core_ids=[0])
    return r.results[0]["out_x"]
```
